# Optimizing a Trainium2 kernel written in Bass

```python
import numpy as np
import jax
import jax.numpy as jnp

def _softmax(x, axis=-1):
    return jax.nn.softmax(x, axis=axis)

def _gelu(x):
    return jax.nn.gelu(x, approximate=True)

def _silu(x):
    return jax.nn.silu(x)

def _sigmoid(x):
    return jax.nn.sigmoid(x)

def _layernorm(x, axis=-1, eps=1e-05):
    m = jnp.mean(x, axis=axis, keepdims=True)
    v = jnp.var(x, axis=axis, keepdims=True)
    return (x - m) / jnp.sqrt(v + eps)

def _scatter_add(tgt, idx, src, axis=0):
    return tgt.at[idx].add(src)

def _segment_sum(src, seg, n):
    return jax.ops.segment_sum(src, seg, n)
kernel_name = 'mk_flamingo_gated_d1_seqx_r4_421739'

def setup_inputs(seed: int=0):
    np.random.seed(seed)
    _w = jnp.asarray

    def _rec_inputs():
        import jax
        import jax.numpy as jnp
        _rk = jax.random.key(seed)
        x = -0.0002928 + 1 * jax.random.normal(jax.random.fold_in(_rk, 1), (2, 1024, 256), jnp.float32)
        _lenS = 1024 - jax.random.randint(jax.random.fold_in(_rk, 7), (2,), 0, max(1, 1024 // 4) + 1, jnp.int32)
        _lenS2 = 77 - jax.random.randint(jax.random.fold_in(_rk, 8), (2,), 0, max(1, 77 // 4) + 1, jnp.int32)
        _ctx_1024P = jax.random.normal(jax.random.fold_in(_rk, 11), (2, 16, 256), jnp.float32)
        _ctx_1024c = jax.random.dirichlet(jax.random.fold_in(_rk, 511), 0.3 * jnp.ones((16,), jnp.float32), (2, 77))
        _ctx_1024t = jnp.einsum('bsk,bkd->bsd', _ctx_1024c, _ctx_1024P)
        _ctx_1024t = _ctx_1024t * jax.lax.rsqrt(jnp.mean(jnp.square(_ctx_1024t)) + 1e-12) * 0.953939
        ctx_1024 = -1.39393e-06 + 0.999914 * (_ctx_1024t + 0.3 * jax.random.normal(jax.random.fold_in(_rk, 611), (2, 77, 256), jnp.float32))
        fside_BxS2_0 = jax.random.uniform(jax.random.fold_in(_rk, 12), (2, 77), jnp.float32, 0.0, 0.999833)
        _g = jax.random.normal(jax.random.fold_in(_rk, 9001), (2, 1), jnp.float32)
        _g = jnp.sign(_g) * jnp.maximum(jnp.abs(_g), 1.0) + (_g == 0) * 1.0
        g_xattn = _g[0]
        g_ffn = _g[1]
        return (x, ctx_1024, fside_BxS2_0, g_xattn, g_ffn)
    x, ctx_1024, fside_BxS2_0, g_xattn, g_ffn = _rec_inputs()

    def _L0_xattn_setup():
        import jax, jax.numpy as jnp
        import numpy as np
        B, NQ, S, D = (2, 512, 512, 256)
        H, HD, OUT = (16, 64, 256)
        key = jax.random.key(seed)
        ks = jax.random.split(key, 8)
        scale = 1.0 / np.sqrt(D)
        return {'queries': jax.random.normal(ks[0], (B, NQ, D), jnp.float32), 'keys': jax.random.normal(ks[1], (B, S, D), jnp.float32), 'values': jax.random.normal(ks[2], (B, S, D), jnp.float32), 'indicators': jax.random.uniform(ks[3], (B, S), jnp.float32), 'Wq': jax.random.normal(ks[4], (D, H * HD), jnp.float32) * scale, 'Wk': jax.random.normal(ks[5], (D, H * HD), jnp.float32) * scale, 'Wv': jax.random.normal(ks[6], (D, H * HD), jnp.float32) * scale, 'Wo': jax.random.normal(ks[7], (H * HD, OUT), jnp.float32) * scale}
    _L0_xattn_all = _L0_xattn_setup()
    _L0_xattn_in = {k: v for k, v in _L0_xattn_all.items() if k in ('Wq', 'Wk', 'Wv', 'Wo')}
    del _L0_xattn_all

    def _L0_ffn_setup():
        import jax, jax.numpy as jnp
        import numpy as np
        B, S, H, F, E = (4, 512, 256, 1024, 8)
        key = jax.random.key(seed)
        ks = jax.random.split(key, 8)
        s = 1.0 / np.sqrt(H)
        sf = 1.0 / np.sqrt(F)
        return {'x': jax.random.normal(ks[0], (B, S, H), jnp.float32), 'wr': jax.random.uniform(ks[1], (H, E), jnp.float32, -s, s), 'br': jax.random.uniform(ks[2], (E,), jnp.float32, -s, s), 'w1': jax.random.uniform(ks[3], (E, H, F), jnp.float32, -s, s), 'b1': jax.random.uniform(ks[4], (E, F), jnp.float32, -s, s), 'w2': jax.random.uniform(ks[5], (E, F, H), jnp.float32, -sf, sf), 'b2': jax.random.uniform(ks[6], (E, H), jnp.float32, -sf, sf)}
    _L0_ffn_all = _L0_ffn_setup()
    _L0_ffn_in = {k: v for k, v in _L0_ffn_all.items() if k in ('wr', 'br', 'w1', 'b1', 'w2', 'b2')}
    del _L0_ffn_all
    return {'x': x, 'ctx_1024': ctx_1024, 'fside_BxS2_0': fside_BxS2_0, 'g_xattn': g_xattn, 'g_ffn': g_ffn, 'L0_xattn_Wq': _L0_xattn_in['Wq'], 'L0_xattn_Wk': _L0_xattn_in['Wk'], 'L0_xattn_Wv': _L0_xattn_in['Wv'], 'L0_xattn_Wo': _L0_xattn_in['Wo'], 'L0_ffn_wr': _L0_ffn_in['wr'], 'L0_ffn_br': _L0_ffn_in['br'], 'L0_ffn_w1': _L0_ffn_in['w1'], 'L0_ffn_b1': _L0_ffn_in['b1'], 'L0_ffn_w2': _L0_ffn_in['w2'], 'L0_ffn_b2': _L0_ffn_in['b2']}

def reference(x, ctx_1024, fside_BxS2_0, g_xattn, g_ffn, L0_xattn_Wq, L0_xattn_Wk, L0_xattn_Wv, L0_xattn_Wo, L0_ffn_wr, L0_ffn_br, L0_ffn_w1, L0_ffn_b1, L0_ffn_w2, L0_ffn_b2):
    import jax
    import jax.numpy as jnp

    def _L0_xattn_ref(queries, keys, values, indicators, Wq, Wk, Wv, Wo):
        import jax, jax.numpy as jnp
        import numpy as np
        B, NQ, S, D = (2, 512, 512, 256)
        H, HD, OUT = (16, 64, 256)
        b, nq, _ = queries.shape
        s = keys.shape[1]
        Q = (queries @ Wq).reshape(b, nq, H, HD).transpose(0, 2, 1, 3)
        K = (keys @ Wk).reshape(b, s, H, HD).transpose(0, 2, 1, 3)
        V = (values @ Wv).reshape(b, s, H, HD).transpose(0, 2, 1, 3)
        scores = jnp.einsum('bhqd,bhkd->bhqk', Q, K) / jnp.sqrt(jnp.float32(HD))
        probs = jax.nn.softmax(scores, axis=-1)
        probs = probs * indicators[:, None, None, :]
        ctx = jnp.einsum('bhqk,bhkd->bhqd', probs, V)
        ctx = ctx.transpose(0, 2, 1, 3).reshape(b, nq, H * HD)
        return ctx @ Wo

    def _L0_ffn_ref(x, wr, br, w1, b1, w2, b2):
        import jax, jax.numpy as jnp
        import numpy as np
        B, S, H, F, E = (4, 512, 256, 1024, 8)
        scores = jnp.einsum('bsh,he->bse', x, wr) + br
        expert_id = jnp.argmax(scores, axis=-1)
        h = jnp.einsum('bsh,ehf->ebsf', x, w1) + b1[:, None, None, :]
        h = jax.nn.gelu(h, approximate=False)
        y = jnp.einsum('ebsf,efh->ebsh', h, w2) + b2[:, None, None, :]
        one_hot = jax.nn.one_hot(expert_id, E, dtype=x.dtype)
        out = jnp.einsum('ebsh,bse->bsh', y, one_hot)
        return out
    x = x + jnp.tanh(g_xattn[0]) * _L0_xattn_ref(_layernorm(x, axis=-1), ctx_1024, ctx_1024, fside_BxS2_0, L0_xattn_Wq, L0_xattn_Wk, L0_xattn_Wv, L0_xattn_Wo)
    x = x + jnp.tanh(g_ffn[0]) * _L0_ffn_ref(_layernorm(x, axis=-1), L0_ffn_wr, L0_ffn_br, L0_ffn_w1, L0_ffn_b1, L0_ffn_w2, L0_ffn_b2)
    return x

_drawn_inputs = setup_inputs


def setup_inputs(seed=0):
    import zlib

    import numpy as np

    out = dict(_drawn_inputs(seed))
    spreads = {}
    factors = {'L0_ffn_b1': 5.142, 'L0_ffn_b2': 3.649}
    for name, (base, spread) in spreads.items():
        noise = np.random.default_rng([zlib.crc32(name.encode()), seed]).standard_normal(out[name].shape)
        drawn = base * np.exp(spread * noise) if base else spread * noise
        out[name] = jnp.asarray(drawn.astype(out[name].dtype))
    for name, factor in factors.items():
        out[name] = (out[name] * factor).astype(out[name].dtype)
    return out
```

```python
import concourse.bass as bass
from concourse import mybir
from contextlib import ExitStack

F32 = mybir.dt.float32
F16 = mybir.dt.float16
BF16 = mybir.dt.bfloat16
I32 = mybir.dt.int32
U32 = mybir.dt.uint32
ALU = mybir.AluOpType
ACT = mybir.ActivationFunctionType
X_AXIS = mybir.AxisListType.X

P = 128
EPS = 1e-5


def gated_cross_attention_then_routed_ffn(nc, x, ctx_in, ind, g_attn, g_ffn, wq, wk, wv, wo,
                                          wr, br, w1, b1, w2, b2, out):
    B, NQ, D = x.shape
    KEYS = ctx_in.shape[1]
    HD = 64
    H = wq.shape[1] // HD
    NE, _, F = w1.shape
    DK = D // P
    FC = F // P
    PAIRS = H // 2
    HK = H * KEYS
    KC = -(-HK // P)
    HKP = KC * P
    T = B * NQ // P
    assert B == 2 and D == 256 and T == 16 and F == 1024 and NE == 8
    HPB = 512 // KEYS
    BANKS = [(h0, min(HPB, H - h0)) for h0 in range(0, H, HPB)]
    NB = len(BANKS)
    PPB = HPB // 2
    SC_A = 64.0
    SC_P = 1024.0
    SC_VW = 16.0
    SC_W1 = 64.0
    SC_W2 = 256.0
    NTOK = B * NQ
    CAP = NTOK + P
    NT = (NTOK + NE * (P - 1)) // P
    RW = D + 4
    PAD_ID = 4095.0
    rowbuf = nc.dram_tensor("rowbuf", (NE * CAP + P, RW), F32, kind="Internal").ap()
    vwbuf = nc.dram_tensor("vwbuf", (B, HK, D), F32, kind="Internal").ap()
    outf = out.rearrange("b n d -> (b n) d")

    ctx = ExitStack()
    with ctx:
        def sb(name, shape, dt):
            return ctx.enter_context(nc.sbuf_tensor(name, shape, dt))

        def sem(name):
            return ctx.enter_context(nc.semaphore(name))

        WE = 2 * F
        WALL = sb("WALL", [P, NE, 4, WE], F16)
        wflat = WALL[:, :, :, :].rearrange("p e q n -> p (e q n)")
        EXP = 4 * WE

        def early(expert, n, off=0):
            a = expert * EXP + 2 * off
            return wflat[:, a:a + 2 * n].bitcast(F32)
        kbd = early(0, PAIRS * B * 2 * KEYS).rearrange("p (a b j k) -> p a b j k", a=PAIRS, b=B, j=2)
        vbd = early(0, PAIRS * B * 2 * KEYS, PAIRS * B * 2 * KEYS)\
            .rearrange("p (a b j k) -> p a b j k", a=PAIRS, b=B, j=2)
        bd_all = early(0, 2 * PAIRS * B * 2 * KEYS)
        wqT = early(0, PAIRS * D, 2 * PAIRS * B * 2 * KEYS).rearrange("p (a d) -> p a d", a=PAIRS)
        xn = early(2, T * D).rearrange("p (t d) -> p t d", t=T)
        xall = early(3, T * D).rearrange("p (t d) -> p t d", t=T)
        vwp = [early(3, KC * D).rearrange("p (c d) -> p c d", c=KC),
               early(2, KC * D).rearrange("p (c d) -> p c d", c=KC)]
        wk_s = early(4, DK * H * HD).rearrange("p (k n) -> p k n", k=DK)
        wv_s = early(4, DK * H * HD, DK * H * HD).rearrange("p (k n) -> p k n", k=DK)
        wq_s = early(5, DK * H * HD).rearrange("p (k n) -> p k n", k=DK)
        wo_s = early(5, PAIRS * D, PAIRS * D).rearrange("p (a d) -> p a d", a=PAIRS)
        A0 = 6 * EXP
        ah = wflat[:, A0:A0 + B * DK * HK].rearrange("p (b k n) -> p b k n", b=B, k=DK)
        al = wflat[:, A0 + B * DK * HK:A0 + 2 * B * DK * HK].rearrange("p (b k n) -> p b k n", b=B, k=DK)
        E0 = A0 + 2 * B * DK * HK
        probs = wflat[:, E0:E0 + 4 * HKP].bitcast(F32).rearrange("p (r n) -> p r n", r=2)
        assert E0 + 4 * HKP <= NE * EXP

        stage = sb("stage", [P, 2, WE], F32)
        vwf = stage[0:KEYS, :, :].rearrange("p r (h d) -> p r h d", d=D)
        row = sb("row", [P, 2, RW], F32)
        ident = sb("ident", [P, P], F32)
        upper = sb("upper", [P, P], BF16)
        ones = sb("ones", [P, P], BF16)
        wr_s = sb("wr_s", [P, DK, NE], F32)
        br_b = sb("br_b", [P, NE], F32)
        b1r = sb("b1r", [NE * FC, P], F32)
        b1c = sb("b1c", [P, NE * FC], F32)
        gates = sb("gates", [P, 4], F32)
        indT = sb("indT", [KEYS, B], F32)
        vsc = sb("vsc", [KEYS, B], F32)
        mv = sb("mv", [P, T, 2], F32)
        rstd1 = sb("rstd1", [P, T], F32)
        nhalf = sb("nhalf", [P, T], F32)
        bst = sb("bst", [P, 6], F32)
        mv2 = sb("mv2", [P, 2], F32)
        ve2 = sb("ve2", [P, 1], F32)
        mx = sb("mx", [P, H], F32)
        nb = sb("nb", [P, H], F32)
        z = sb("z", [P, 2, H], F32)
        rz = sb("rz", [P, 2, H], F32)
        sc8 = sb("sc8", [P, NE], F32)
        top8 = sb("top8", [P, NE], F32)
        idx8 = sb("idx8", [P, NE], U32)
        idxf = sb("idxf", [P, 1], F32)
        iota8 = sb("iota8", [P, NE], F32)
        onehot = sb("onehot", [P, NE], BF16)
        seen = sb("seen", [P, NE], BF16)
        junk8 = sb("junk8", [P, NE], F32)
        rank = sb("rank", [P, 1], F32)
        pos = sb("pos", [P, 2, 1], I32)
        ids = sb("ids", [P, 2, 1], I32)
        k128 = sb("k128", [P, NE, T], F32)
        incl = sb("incl", [P, NE, NE], F32)
        jrow = sb("jrow", [P, NT, NE], F32)
        ecap = sb("ecap", [P, NE], F32)
        tA = sb("tA", [P, NT * NE], F32)
        tB = sb("tB", [P, NT * NE], F32)
        nt_e = sb("nt_e", [P, NE], F32)
        cum_e = sb("cum_e", [P, NE], F32)
        ej = sb("ej", [P, NT], F32)
        sj = sb("sj", [P, NT], F32)
        kj = sb("kj", [P, NT], F32)
        vj = sb("vj", [P, NT], F32)
        etab = sb("etab", [P, NT], I32)
        rtab = sb("rtab", [P, NT], I32)
        ptab = sb("ptab", [P, NE], I32)
        sc1 = ctx.enter_context(nc.sbuf_tensor("padrow", [P, RW], F32))

        inner = ExitStack()

        def sbi(name, shape, dt):
            return inner.enter_context(nc.sbuf_tensor(name, shape, dt))
        xth = sbi("xth", [P, DK, T * P], F16)
        xtl = sbi("xtl", [P, DK, T * P], F16)
        vwh = sbi("vwh", [P, B, KC, D], F16)
        vwl = sbi("vwl", [P, B, KC, D], F16)
        pth = sbi("pth", [P, 2, KC, P], F16)
        ptl = sbi("ptl", [P, 2, KC, P], F16)
        xr = sbi("xr", [P, 2, D], F32)
        xn2 = sbi("xn2", [P, D], F32)
        xt2 = sbi("xt2", [P, DK, P], F32)
        ctx_s = sbi("ctx_s", [KEYS, B, D], F32)
        ctxT = sbi("ctxT", [P, DK, B * KEYS], F32)
        inner.close()
        inner = ExitStack()
        b2t = sbi("b2t", [P, NE, D], F32)
        ra = sbi("ra", [P, 2, RW], F32)
        rb = sbi("rb", [P, 2, RW], F32)
        xnf = sbi("xnf", [P, 2, D], F32)
        fxh = sbi("fxh", [P, 2, DK, P], F16)
        fxl = sbi("fxl", [P, 2, DK, P], F16)
        hid = sbi("hid", [P, 2, FC, P], F32)
        hh = sbi("hh", [P, 2, FC, P], F16)
        hl = sbi("hl", [P, 2, FC, P], F16)
        yt = sbi("yt", [P, D], F32)
        yo = sbi("yo", [P, 2, D], F32)
        inner.close()

        ps = [ctx.enter_context(nc.psum_tensor(f"ps{i}", [P, 512], F32)) for i in range(8)]
        S = ps[0:NB]
        PT = ps[3:6]
        O = ps[6]
        R = ps[7]
        RT, RS, RP = R[:, 0:D], R[:, D:D + NE], R[:, D + NE:D + 2 * NE]
        CPB = 4
        PTB = [(c0, min(CPB, KC - c0)) for c0 in range(0, KC, CPB)]

        ld_ctx, ld_wk, ld_wv, ld_wq, ld_wo = (sem(n) for n in ("ld_ctx", "ld_wk", "ld_wv", "ld_wq", "ld_wo"))
        ld_x = [sem("ld_x0"), sem("ld_x1")]
        ld_small = sem("ld_small")
        ld_b1 = sem("ld_b1")
        consts = sem("consts")
        passed = sem("passed")
        const_id = sem("const_id")
        bd_zero = sem("bd_zero")
        filled = sem("filled")
        act_out = sem("act_out")
        dve_out = sem("dve_out")
        gate_ok = sem("gate_ok")
        vsc_ok = sem("vsc_ok")
        ln1_st = sem("ln1_st")
        ln1_mv = sem("ln1_mv")
        ln1_ve = sem("ln1_ve")
        ln1_rs = sem("ln1_rs")
        ln1_xn = sem("ln1_xn")
        vw_st = [sem("vw_st0"), sem("vw_st1")]
        vw_ld = [sem("vw_ld0"), sem("vw_ld1")]
        vw_hi = sem("vw_hi")
        vw_lo = sem("vw_lo")
        s_sc = sem("s_sc")
        s_mx = sem("s_mx")
        s_nb = sem("s_nb")
        s_ex = sem("s_ex")
        ids_ok = sem("ids_ok")
        s_rz = sem("s_rz")
        s_nm = sem("s_nm")
        s_pt = sem("s_pt")
        s_ph = sem("s_ph")
        s_pl = sem("s_pl")
        s_pv = sem("s_pv")
        s_x2 = sem("s_x2")
        s_bs = sem("s_bs")
        s_ag = sem("s_ag")
        s_ve = sem("s_ve")
        s_rs = sem("s_rs")
        s_nr = sem("s_nr")
        s_xn = sem("s_xn")
        s_t2 = sem("s_t2")
        s_tc = sem("s_tc")
        s_ro = sem("s_ro")
        s_sb = sem("s_sb")
        s_tp = sem("s_tp")
        s_ix = sem("s_ix")
        s_if = sem("s_if")
        s_oh = sem("s_oh")
        s_px = sem("s_px")
        s_rk = sem("s_rk")
        s_po = sem("s_po")
        s_ct = sem("s_ct")
        sct = [sem("sct0"), sem("sct1")]
        ld_xr = [sem("ld_xr0"), sem("ld_xr1")]
        ld_st = [sem("ld_st0"), sem("ld_st1")]
        s_wh = sem("s_wh")
        s_wl = sem("s_wl")
        pad0 = sem("pad0")
        padded = sem("padded")
        ld_b2 = sem("ld_b2")
        tab = sem("tab")
        tabs_ok = sem("tabs_ok")
        n_ok = sem("n_ok")
        ld_ra = [sem("ld_ra0"), sem("ld_ra1")]
        ld_rb = [sem("ld_rb0"), sem("ld_rb1")]
        f_xn = sem("f_xn")
        f_xt = sem("f_xt")
        f_xh = sem("f_xh")
        f_xl = sem("f_xl")
        f_h = sem("f_h")
        f_ge = sem("f_ge")
        f_hh = sem("f_hh")
        f_hl = sem("f_hl")
        f_y = sem("f_y")
        f_t1 = sem("f_t1")
        f_yo = sem("f_yo")
        f_id = sem("f_id")
        f_sc = [sem("f_sc0"), sem("f_sc1")]

        block = ctx.enter_context(nc.Block())

        NCONSTS = 13

        def wait(eng, s, v):
            if not isinstance(v, int) or v > 0:
                eng.wait_ge(s, v)

        def wait_apart(eng, s, v):
            wait(eng, s, v)
            eng.sem_inc(passed, 1)

        LAG = 5
        PEEL = 6

        def steps(eng, body):
            for s in range(PEEL):
                body(s, s % 2)
            with eng.Fori(PEEL // 2, T // 2) as q:
                body(2 * q, 0)
                body(2 * q + 1, 1)
            for s in range(T, T + LAG):
                body(s, s % 2)

        def has(s, lag):
            return not isinstance(s, int) or 0 <= s - lag < T

        FLAG = 4
        FPEEL = 6

        def fsteps(eng, body):
            for s in range(FPEEL):
                body(s, s % 2)
            with eng.Fori(FPEEL // 2, NT // 2) as q:
                body(2 * q, 0)
                body(2 * q + 1, 1)
            for s in range(NT - NT % 2, NT + FLAG):
                body(s, s % 2)

        def fhas(s, lag):
            return not isinstance(s, int) or 0 <= s - lag < NT

        WLAG = 4
        NP = 2 * NE

        def has_piece(s):
            return not isinstance(s, int) or 0 <= s - WLAG < NP

        fills = [("ctxT", 0, "D")]
        fills += [("k", g, "D") for g in range(NB)]
        fills += [("wqT", g, "AD"[g % 2]) for g in range(4)]
        fills += [("b1", 0, "D")]
        fills += [("a", (b, k, g), "D") for b in range(B) for k in range(DK) for g in range(NB)]
        fills += [("x", g, "D") for g in range(T // 2)]
        fills += [("v", g, "D") for g in range(NB)]
        fills += [("vw", (b, i), "AD"[i % 2]) for b in range(B) for i in range(PAIRS)]
        released = []
        n_rel = {"A": 0, "D": 0}
        for kind, _, who in fills:
            n_rel[who] += 1
            released.append((who, n_rel[who]))
        hi_done = sem("hi_done")
        his = {}
        for n, (kind, _, _) in enumerate(fills):
            if kind in ("a", "x"):
                his[n] = len(his) + 1
        of_kind = {}
        for n, (kind, arg, _) in enumerate(fills):
            of_kind.setdefault(kind, []).append(n)

        def emptied(eng, n):
            who, v = released[n]
            eng.wait_ge(act_out if who == "A" else dve_out, v)

        def all_emptied(eng, kind):
            for who in "AD":
                v = max([released[n][1] for n in of_kind[kind] if released[n][0] == who], default=0)
                if v:
                    eng.wait_ge(act_out if who == "A" else dve_out, v)

        @block.sync
        def _(sp):
            sp.dma_start(ctx_s[:, :, :], ctx_in.rearrange("b k d -> k b d")).then_inc(ld_ctx, 16)
            sp.dma_start(wk_s, wk.rearrange("(k p) n -> p k n", p=P)).then_inc(ld_wk, 16)
            xv = x.rearrange("b (n p) d -> p n b d", p=P)
            xa = xall.rearrange("p (n b) d -> p n b d", b=B)
            sp.dma_start(wq_s, wq.rearrange("(k p) n -> p k n", p=P)).then_inc(ld_wq, 16)
            for i in range(2):
                for b in range(B):
                    sp.dma_start(xa[:, i * T // 4:(i + 1) * T // 4, b, :],
                                 xv[:, i * T // 4:(i + 1) * T // 4, b, :]).then_inc(ld_x[i], 16)
            sp.dma_start(wv_s, wv.rearrange("(k p) n -> p k n", p=P)).then_inc(ld_wv, 16)
            sp.dma_start(wo_s, wo.rearrange("(a p) d -> p a d", p=P)).then_inc(ld_wo, 16)
            vws = [vwbuf[b].rearrange("(h k) d -> k h d", h=H) for b in range(B)]
            vwn = of_kind["vw"]
            for b in range(B):
                for half in range(2):
                    last = vwn[b * PAIRS + half * PAIRS // 2 + PAIRS // 2 - 1]
                    emptied(sp, last)
                    emptied(sp, last - 1)
                    sp.dma_start(vws[b][:, half * H // 2:(half + 1) * H // 2, :],
                                 vwf[:, half, :, :]).then_inc(vw_st[half], 16)
            for b in range(B):
                for half in range(2):
                    sp.wait_ge(vw_st[half], 16 * (b + 1))
                full = HK // P
                all_emptied(sp, "x")
                sp.dma_start(vwp[b][:, 0:full, :],
                             vwbuf[b, 0:full * P, :].rearrange("(c p) d -> p c d", p=P)).then_inc(vw_ld[b], 16)
                sp.dma_start(vwp[b][0:HK - full * P, full, :], vwbuf[b, full * P:HK, :]).then_inc(vw_ld[b], 16)

            def body(s, par):
                if has(s, 3):
                    t = s - 3
                    wait(sp, s_x2, t - 1)
                    bt = 1 - par
                    if isinstance(s, int):
                        src = x[bt, (t // 2) * P:(t // 2 + 1) * P, :]
                    else:
                        src = x[bt, bass.ds((t - bt) * (P // 2), P), :]
                    sp.dma_start(xr[:, 1 - par, :], src).then_inc(ld_xr[1 - par], 16)
                if has_piece(s + 1):
                    p = s + 1 - WLAG
                    pp = 1 - par
                    wait(sp, s_wh, p - 1)
                    wait(sp, s_wl, p - 1)
                    if isinstance(s, int):
                        w1e, w2e = w1[p // 2], w2[p // 2]
                    else:
                        w1e = w1.rearrange("e d f -> (e d) f")[bass.ds((p - pp) * (D // 2), D), :]
                        w2e = w2.rearrange("e f d -> (e f) d")[bass.ds((p - pp) * (F // 2), F), :]
                    if pp == 0:
                        sp.dma_start(stage[:, 0, :].rearrange("p (k n) -> p k n", k=DK),
                                     w1e.rearrange("(k p) n -> p k n", p=P)).then_inc(ld_st[0], 16)
                    else:
                        sp.dma_start(stage[:, 1, :].rearrange("p (c d) -> p c d", c=FC),
                                     w2e.rearrange("(c p) d -> p c d", p=P)).then_inc(ld_st[1], 16)
            steps(sp, body)
            sp.wait_ge(s_pv, T)
            sp.wait_ge(s_ro, T)
            sp.dma_start(b2t[:, :, :].rearrange("p e d -> p (e d)"),
                         b2.rearrange("e d -> (e d)").unsqueeze(0).to_broadcast([P, NE * D])).then_inc(ld_b2, 16)
            sp.wait_ge(pad0, 1)
            sp.wait_ge(tabs_ok, 1)
            sp.dma_start(rowbuf[NE * CAP:NE * CAP + P, :], sc1[:, :]).then_inc(padded, 16)
            with sp.Fori(0, NE) as e:
                r = sp.value_load(ptab[0:1, bass.ds(e, 1)], min_val=0, max_val=NE * CAP)
                sp.dma_start(rowbuf[bass.ds(r, P), :], sc1[:, :]).then_inc(padded, 16)
            sp.wait_ge(padded, 16 * (NE + 1))
            for i in range(2):
                sp.wait_ge(sct[i], 16 * T // 2)

            def fbody(s, par):
                if fhas(s, 0):
                    wait(sp, f_xn, s - 1)
                    r = sp.value_load(rtab[0:1, bass.ds(s, 1)], min_val=0, max_val=NE * CAP)
                    sp.dma_start(ra[:, par, :], rowbuf[bass.ds(r, P), :]).then_inc(ld_ra[par], 16)
                if fhas(s, 3):
                    t = s - 3
                    wait(sp, f_yo, t - 1)
                    wait(sp, f_id, t - 1)
                    r = sp.value_load(rtab[0:1, bass.ds(t, 1)], min_val=0, max_val=NE * CAP)
                    sp.dma_start(rb[:, 1 - par, :], rowbuf[bass.ds(r, P), :]).then_inc(ld_rb[1 - par], 16)
            fsteps(sp, fbody)

        @block.gpsimd
        def _(pool):
            pool.memset(ident[:, :], 0.0).then_inc(const_id, 1)
            pool.memset(upper[:, :], 1.0).then_inc(const_id, 1)
            pool.memset(incl[:, :, :], 1.0).then_inc(const_id, 1)
            pool.wait_ge(const_id, 3)
            pool.affine_select(out=ident[:, :], in_=ident[:, :], compare_op=ALU.not_equal, fill=1.0,
                               base=0, pattern=[[-1, P]], channel_multiplier=1).then_inc(consts, 1)
            pool.affine_select(out=upper[:, :], in_=upper[:, :], compare_op=ALU.is_gt, fill=0.0,
                               base=0, pattern=[[1, P]], channel_multiplier=-1).then_inc(consts, 1)
            pool.affine_select(out=incl[:, :, :], in_=incl[:, :, :], compare_op=ALU.is_ge, fill=0.0,
                               base=0, pattern=[[1, NE], [-1, NE]], channel_multiplier=0).then_inc(consts, 1)
            pool.memset(ones[:, :], 1.0).then_inc(consts, 1)
            pool.memset(seen[:, :], 0.0).then_inc(consts, 1)
            pool.memset(nhalf[:, :], -0.5).then_inc(consts, 1)
            iota = lambda dst, pattern, base, cm: pool.iota(
                dst, pattern, base=base, channel_multiplier=cm,
                allow_small_or_imprecise_dtypes=True).then_inc(consts, 1)
            iota(iota8[:, :], [[1, NE]], 0, 0)
            iota(k128[:, :, :], [[0, NE], [P, T]], 0, 0)
            iota(jrow[:, :, :], [[1, NT], [0, NE]], 0, 0)
            iota(ecap[:, :], [[CAP, NE]], 0, 0)
            for r in range(2):
                iota(row[:, r, D + 2:D + 3], [[0, 1]], r * NQ - P, 1)
            pool.memset(row[:, :, D + 3:D + 4], 0.0).then_inc(consts, 1)
            pool.memset(sc1[:, :], 0.0).then_inc(const_id, 1)
            pool.wait_ge(const_id, 4)
            pool.memset(sc1[:, D + 2:D + 3], PAD_ID).then_inc(pad0, 1)
            pool.wait_ge(ln1_ve, 1)
            pool.tensor_tensor(rstd1[:, 0:T // 2], rstd1[:, 0:T // 2], nhalf[:, 0:T // 2], ALU.pow)\
                .then_inc(ln1_rs, 1)
            pool.wait_ge(ln1_ve, 2)
            pool.tensor_tensor(rstd1[:, T // 2:T], rstd1[:, T // 2:T], nhalf[:, T // 2:T], ALU.pow)\
                .then_inc(ln1_rs, 1)

            def body(s, par):
                if has(s, 4):
                    pool.wait_ge(s_ve, s - 4 + 1)
                    pool.tensor_tensor(row[:, par, D:D + 1], ve2[:, :], nhalf[:, 0:1], ALU.pow).then_inc(s_rs, 1)
                if has(s, 1):
                    pool.wait_ge(s_rz, s - 1 + 1)
                    pv = probs[:, 1 - par, 0:HK].rearrange("p (h k) -> p h k", h=H)
                    pool.tensor_tensor(pv, pv, rz[:, 1 - par, :].unsqueeze(2).to_broadcast([P, H, KEYS]),
                                       ALU.mult).then_inc(s_nm, 1)
                if has(s, 5):
                    wait_apart(pool, s_po, s - 5 + 1)
                    pool.indirect_dma_start(rowbuf[:, :], bass.IndirectOffsetOnAxis(pos[:, 1 - par, :], 0),
                                            row[:, 1 - par, :], None).then_inc(sct[1 - par], 16)
            steps(pool, body)

            def fbody(s, par):
                if fhas(s, 2):
                    t = s - 2
                    pool.wait_ge(f_hh, t + 1)
                    wait(pool, f_y, t - 1)
                    pool.tensor_tensor(hl[:, par, :, :], hid[:, par, :, :], hh[:, par, :, :],
                                       ALU.subtract).then_inc(f_hl, 1)
                if fhas(s, 4):
                    pool.wait_ge(f_id, s - 4 + 1)
                    pool.wait_ge(f_yo, s - 4 + 1)
                    pool.sem_inc(passed, 1)
                    pool.indirect_dma_start(outf[:, :], bass.IndirectOffsetOnAxis(ids[:, par, :], 0),
                                            yo[:, par, :], None, bounds_check=NTOK - 1,
                                            oob_is_err=False).then_inc(f_sc[par], 16)
            fsteps(pool, fbody)
            for i in range(2):
                pool.wait_ge(f_sc[i], 16 * ((NT + 1 - i) // 2))

        @block.scalar
        def _(act):
            act.dma_start(gates[:, 0:1], g_attn.unsqueeze(0).to_broadcast([P, 1])).then_inc(ld_small, 16)
            act.dma_start(gates[:, 1:2], g_ffn.unsqueeze(0).to_broadcast([P, 1])).then_inc(ld_small, 16)
            with nc.allow_non_contiguous_dma(reason="154 values, keys on partitions"):
                act.dma_start(indT[:, :], ind.rearrange("b k -> k b")).then_inc(ld_small, 16)
            act.dma_start(wr_s[:, :, :], wr.rearrange("(k p) e -> p k e", p=P)).then_inc(ld_small, 16)
            act.dma_start(br_b[:, :], br.unsqueeze(0).to_broadcast([P, NE])).then_inc(ld_small, 16)
            act.dma_start(b1r[:, :], b1.rearrange("e (c p) -> (e c) p", p=P)).then_inc(ld_b1, 16)
            act.wait_ge(ld_small, 80)
            act.activation(gates[:, 2:4], gates[:, 0:2], ACT.Tanh).then_inc(gate_ok, 1)
            for n, (kind, arg, who) in enumerate(fills):
                bank = ps[n % 8]
                if kind == "k" or kind == "v":
                    pass
                elif kind == "wqT" and who == "A":
                    act.wait_ge(filled, n + 1)
                    act.activation(wqT[:, 2 * arg:2 * arg + 2, :].rearrange("p a d -> p (a d)"),
                                   bank[:, :], ACT.Copy).then_inc(act_out, 1)
                elif kind == "a":
                    b, k, g = arg
                    h0, nh = BANKS[g]
                    act.wait_ge(filled, n + 1)
                    act.activation(ah[:, b, k, h0 * KEYS:(h0 + nh) * KEYS], bank[:, 0:nh * KEYS],
                                   ACT.Copy, scale=SC_A / HD ** 0.5).then_inc(hi_done, 1)
                elif kind == "x":
                    act.wait_ge(filled, n + 1)
                    act.activation(xth[:, :, 2 * arg * P:(2 * arg + 2) * P],
                                   bank[:, :].rearrange("p (k m) -> p k m", k=DK), ACT.Copy).then_inc(hi_done, 1)
                elif kind == "vw" and who == "A":
                    b, i = arg
                    half = i // (PAIRS // 2)
                    if b:
                        act.wait_ge(vw_st[half], 16 * b)
                    act.wait_ge(filled, n + 1)
                    act.wait_ge(vsc_ok, 1)
                    j = 2 * (i % (PAIRS // 2))
                    act.activation(vwf[:, half, j:j + 2, :].rearrange("p h d -> p (h d)"), bank[0:KEYS, :],
                                   ACT.Copy, scale=vsc[:, b:b + 1]).then_inc(act_out, 1)
            for b in range(B):
                act.wait_ge(vw_ld[b], 32)
                act.activation(vwh[:, b, :, :], vwp[b], ACT.Copy).then_inc(vw_hi, 1)

            def body(s, par):
                if has(s, 0):
                    act.wait_ge(s_nb, s + 1)
                    wait(act, s_pt, NB * (s - 1))
                    wait(act, s_rz, s - 1)
                    for g, (h0, nh) in enumerate(BANKS):
                        for h in range(h0, h0 + nh):
                            ins = act.activation(probs[:, par, h * KEYS:(h + 1) * KEYS],
                                                 S[g][:, (h - h0) * KEYS:(h - h0 + 1) * KEYS], ACT.Exp,
                                                 bias=nb[:, h:h + 1], scale=1.0 / SC_A,
                                                 accum_out=z[:, par, h:h + 1])
                        ins.then_inc(s_ex, 1)
                if has(s, 2):
                    t = s - 2
                    wait(act, s_pv, t - 1)
                    for g, (c0, n) in enumerate(PTB):
                        act.wait_ge(s_pt, NB * t + g + 1)
                        act.activation(pth[:, par, c0:c0 + n, :].rearrange("p c m -> p (c m)"),
                                       PT[g][:, 0:n * P], ACT.Copy, scale=SC_P).then_inc(s_ph, 1)
                if has(s, 4):
                    act.wait_ge(s_t2, s - 4 + 1)
                    wait(act, s_ro, s - 4)
                    act.activation(xt2[:, :, :].rearrange("p k m -> p (k m)"), RT, ACT.Copy).then_inc(s_tc, 1)
                if has_piece(s):
                    p = s - WLAG
                    if isinstance(s, int) and s >= T:
                        act.wait_ge(s_sc, NB * T)
                        act.wait_ge(s_pt, NB * min(T, s - 1))
                    act.wait_ge(ld_st[par], 16 * ((p - par) // 2 + 1) if isinstance(s, int)
                                else (p - par) * 8 + 16)
                    dst = wflat[:, bass.ds((p - par) * (EXP // 2) + par * 2 * WE, WE)]
                    act.activation(dst, stage[:, par, :], ACT.Copy, scale=(SC_W1, SC_W2)[par]).then_inc(s_wh, 1)
            steps(act, body)

            def fbody(s, par):
                if fhas(s, 1):
                    t = s - 1
                    act.wait_ge(f_xt, t + 1)
                    wait(act, f_h, 2 * (t - 1))
                    act.activation(fxh[:, 1 - par, :, :].rearrange("p k m -> p (k m)"), ps[1 - par][:, 0:D],
                                   ACT.Copy).then_inc(f_xh, 1)
                if fhas(s, 2):
                    t = s - 2
                    e = act.value_load(etab[0:1, bass.ds(t, 1)], min_val=0, max_val=NE - 1)
                    wait(act, f_hl, t - 1)
                    for g in range(2):
                        act.wait_ge(f_h, 2 * t + g + 1)
                        for c in range(FC // 2):
                            cc = g * FC // 2 + c
                            ins = act.activation(hid[:, par, cc, :], ps[2 + 2 * par + g][:, c * P:(c + 1) * P],
                                                 ACT.Gelu, bias=b1c[:, bass.ds(e * FC + cc, 1)],
                                                 scale=1.0 / SC_W1)
                        ins.then_inc(f_ge, 1)
            fsteps(act, fbody)

        @block.tensor
        def _(pe):
            pe.wait_ge(consts, NCONSTS)
            for n, (kind, arg, who) in enumerate(fills):
                bank = ps[n % 8]
                if n >= 8:
                    emptied(pe, n - 8)
                if kind == "ctxT":
                    pe.wait_ge(ld_ctx, 16)
                    for k in range(DK):
                        for b in range(B):
                            c = (k * B + b) * KEYS
                            ins = pe.transpose(bank[:, c:c + KEYS], ctx_s[:, b, k * P:(k + 1) * P],
                                               ident[0:KEYS, 0:KEYS])
                elif kind in "kv":
                    if arg == 0:
                        emptied(pe, of_kind["ctxT"][0])
                        pe.wait_ge(ld_wk if kind == "k" else ld_wv, 16)
                    w = wk_s if kind == "k" else wv_s
                    pairs = range(arg * PPB, min((arg + 1) * PPB, PAIRS))
                    for i, a in enumerate(pairs):
                        for k in range(DK):
                            ins = pe.matmul(bank[:, i * B * KEYS:(i + 1) * B * KEYS],
                                            w[:, k, a * P:(a + 1) * P], ctxT[:, k, :],
                                            start=(k == 0), stop=(k == DK - 1))
                elif kind == "wqT":
                    if arg == 0:
                        pe.wait_ge(ld_wq, 16)
                    for i in range(2):
                        for k in range(DK):
                            a = 2 * arg + i
                            ins = pe.transpose(bank[:, (i * DK + k) * P:(i * DK + k + 1) * P],
                                               wq_s[:, k, a * P:(a + 1) * P], ident[:, :])
                elif kind == "b1":
                    pe.wait_ge(ld_b1, 16)
                    ins = pe.transpose(bank[:, 0:NE * FC], b1r[:, :], ident[0:NE * FC, 0:NE * FC])
                elif kind == "a":
                    b, k, g = arg
                    if n == of_kind["a"][0]:
                        all_emptied(pe, "wqT")
                        all_emptied(pe, "k")
                    for i, a in enumerate(range(g * PPB, min((g + 1) * PPB, PAIRS))):
                        ins = pe.matmul(bank[:, i * 2 * KEYS:(i + 1) * 2 * KEYS], wqT[:, a, k * P:(k + 1) * P],
                                        kbd[:, a, b, :, :].rearrange("p j k -> p (j k)"), start=True, stop=True)
                elif kind == "x":
                    pe.wait_ge(ln1_xn, 2 * arg + 2)
                    for k in range(DK):
                        for i in range(2):
                            ins = pe.transpose(bank[:, (k * 2 + i) * P:(k * 2 + i + 1) * P],
                                               xn[:, 2 * arg + i, k * P:(k + 1) * P], ident[:, :])
                elif kind == "vw":
                    b, a = arg
                    if n == of_kind["vw"][0]:
                        all_emptied(pe, "v")
                        pe.wait_ge(ld_wo, 16)
                    for j in range(2):
                        ins = pe.matmul(bank[0:KEYS, j * D:(j + 1) * D], vbd[:, a, b, j, :], wo_s[:, a, :],
                                        start=True, stop=True)
                ins.then_inc(filled, 1)
            for n in range(len(fills) - 8, len(fills)):
                emptied(pe, n)

            def body(s, par):
                if has(s, 0):
                    xs = bass.ds(s * P, P)
                    for g, (h0, nh) in enumerate(BANKS):
                        cols = slice(h0 * KEYS, (h0 + nh) * KEYS)
                        wait(pe, s_ex, NB * (s - 1) + g + 1)
                        for k in range(DK):
                            for i, (l, r) in enumerate(((xth, ah), (xth, al), (xtl, ah))):
                                ins = pe.matmul(S[g][:, 0:nh * KEYS], l[:, k, xs], r[:, par, k, cols],
                                                start=(k == 0 and i == 0), stop=(k == DK - 1 and i == 2))
                        ins.then_inc(s_sc, 1)
                if has(s, 5):
                    t = s - 5
                    pe.wait_ge(s_oh, t + 1)
                    pe.matmul(RP, upper[:, :], onehot[:, :], start=True, stop=False)
                    pe.matmul(RP, ones[:, :], seen[:, :], start=False, stop=True).then_inc(s_px, 1)
                if has(s, 2):
                    t = s - 2
                    pe.wait_ge(s_nm, t + 1)
                    for g, (c0, n) in enumerate(PTB):
                        wait(pe, s_pl, NB * (t - 1) + g + 1)
                        for i in range(n):
                            c = c0 + i
                            ins = pe.transpose(PT[g][:, i * P:(i + 1) * P], probs[:, par, c * P:(c + 1) * P],
                                               ident[:, :])
                        ins.then_inc(s_pt, 1)
                if has(s, 4):
                    t = s - 4
                    pe.wait_ge(s_xn, t + 1)
                    wait(pe, s_rk, t)
                    for k in range(DK):
                        ins = pe.transpose(R[:, k * P:(k + 1) * P], xn2[:, k * P:(k + 1) * P], ident[:, :])
                    ins.then_inc(s_t2, 1)
                if has(s, 3):
                    t = s - 3
                    wait(pe, s_x2, t)
                    pb = 1 - par
                    for g, (c0, n) in enumerate(PTB):
                        pe.wait_ge(s_pl, NB * t + g + 1)
                        for c in range(c0, c0 + n):
                            for i, (l, r) in enumerate(((pth, vwh), (pth, vwl), (ptl, vwh))):
                                ins = pe.matmul(O[:, 0:D], l[:, pb, c, :], r[:, pb, c, :],
                                                start=(c == 0 and i == 0), stop=(c == KC - 1 and i == 2))
                    ins.then_inc(s_pv, 1)
                if has(s, 4):
                    t = s - 4
                    pe.wait_ge(s_tc, t + 1)
                    for k in range(DK):
                        ins = pe.matmul(RS, xt2[:, k, :], wr_s[:, k, :], start=(k == 0), stop=(k == DK - 1))
                    ins.then_inc(s_ro, 1)
            steps(pe, body)
            pe.wait_ge(s_ct, T)
            pe.matmul(RP, ones[:, :], seen[:, :], start=True, stop=True).then_inc(n_ok, 1)
            pe.wait_ge(tabs_ok, 1)

            def fbody(s, par):
                if fhas(s, 1):
                    t = s - 1
                    pe.wait_ge(f_xn, t + 1)
                    wait(pe, f_xl, t - 1)
                    for k in range(DK):
                        ins = pe.transpose(ps[1 - par][:, k * P:(k + 1) * P], xnf[:, 1 - par, k * P:(k + 1) * P],
                                           ident[:, :])
                    ins.then_inc(f_xt, 1)
                if fhas(s, 2):
                    t = s - 2
                    e = pe.value_load(etab[0:1, bass.ds(t, 1)], min_val=0, max_val=NE - 1)
                    pe.wait_ge(f_xl, t + 1)
                    wait(pe, f_ge, 2 * (t - 1))
                    for c in range(FC):
                        hb = ps[2 + 2 * par + c // (FC // 2)]
                        dst = hb[:, (c % (FC // 2)) * P:(c % (FC // 2) + 1) * P]
                        for k in range(DK):
                            for i, (q, r) in enumerate(((0, fxh), (0, fxl), (1, fxh))):
                                ins = pe.matmul(dst, wflat[:, bass.ds(e * EXP + (q * WE + k * F + c * P), P)],
                                                r[:, par, k, :],
                                                start=(k == 0 and i == 0), stop=(k == DK - 1 and i == 2))
                        if c % (FC // 2) == FC // 2 - 1:
                            ins.then_inc(f_h, 1)
                if fhas(s, 3):
                    t = s - 3
                    e = pe.value_load(etab[0:1, bass.ds(t, 1)], min_val=0, max_val=NE - 1)
                    pb = 1 - par
                    pe.wait_ge(f_hl, t + 1)
                    wait(pe, f_yo, t - 1)
                    for c in range(FC):
                        for i, (l, q) in enumerate(((hh, 2), (hh, 3), (hl, 2))):
                            ins = pe.matmul(ps[6 + pb][:, 0:D], l[:, pb, c, :],
                                            wflat[:, bass.ds(e * EXP + (q * WE + c * D), D)],
                                            start=(c == 0 and i == 0), stop=(c == FC - 1 and i == 2))
                    ins.then_inc(f_y, 1)
            fsteps(pe, fbody)

        @block.vector
        def _(dve):
            dve.memset(bd_all, 0.0).then_inc(bd_zero, 1)
            dve.wait_ge(bd_zero, 1)

            def evacuate(n):
                kind, arg, who = fills[n]
                if who != "D":
                    return
                bank = ps[n % 8]
                dve.wait_ge(filled, n + 1)
                if kind == "ctxT":
                    ins = dve.tensor_copy(ctxT[:, :, :].rearrange("p k m -> p (k m)"), bank[:, 0:DK * B * KEYS])
                elif kind in "kv":
                    bd = kbd if kind == "k" else vbd
                    a0, a1 = arg * PPB, min((arg + 1) * PPB, PAIRS)
                    for j in range(2):
                        rows = slice(j * HD, (j + 1) * HD)
                        ins = dve.tensor_copy(bd[rows, a0:a1, :, j, :],
                                              bank[rows, 0:(a1 - a0) * B * KEYS].rearrange(
                                                  "p (a b k) -> p a b k", b=B, k=KEYS))
                elif kind == "wqT":
                    ins = dve.tensor_copy(wqT[:, 2 * arg:2 * arg + 2, :].rearrange("p a d -> p (a d)"), bank[:, :])
                elif kind == "b1":
                    ins = dve.tensor_copy(b1c[:, :], bank[:, 0:NE * FC])
                elif kind == "a":
                    b, k, g = arg
                    h0, nh = BANKS[g]
                    cols = slice(h0 * KEYS, (h0 + nh) * KEYS)
                    dve.wait_ge(hi_done, his[n])
                    ins = dve.scalar_tensor_tensor(al[:, b, k, cols], bank[:, 0:nh * KEYS], SC_A / HD ** 0.5,
                                                   ah[:, b, k, cols], ALU.mult, ALU.subtract)
                elif kind == "x":
                    m = slice(2 * arg * P, (2 * arg + 2) * P)
                    dve.wait_ge(hi_done, his[n])
                    ins = dve.tensor_tensor(xtl[:, :, m], bank[:, :].rearrange("p (k m) -> p k m", k=DK),
                                            xth[:, :, m], ALU.subtract)
                elif kind == "vw":
                    b, i = arg
                    half = i // (PAIRS // 2)
                    if b:
                        dve.wait_ge(vw_st[half], 16 * b)
                    j = 2 * (i % (PAIRS // 2))
                    ins = dve.tensor_scalar(vwf[:, half, j:j + 2, :].rearrange("p h d -> p (h d)"),
                                            bank[0:KEYS, :], vsc[:, b:b + 1], None, ALU.mult)
                ins.then_inc(dve_out, 1)

            for n in range(of_kind["a"][0]):
                evacuate(n)
            for i in range(2):
                dve.wait_ge(ld_x[i], 32)
                for t in range(i * T // 2, (i + 1) * T // 2):
                    wait(dve, ln1_mv, t)
                    dve.bn_stats(bst[:, :], xall[:, t, :]).then_inc(ln1_st, 1)
                    dve.wait_ge(ln1_st, t + 1)
                    dve.bn_aggr(mv[:, t, :], bst[:, :]).then_inc(ln1_mv, 1)
                h = slice(i * T // 2, (i + 1) * T // 2)
                dve.wait_ge(ln1_mv, (i + 1) * T // 2)
                dve.tensor_scalar(rstd1[:, h], mv[:, h, 1], EPS, None, ALU.add).then_inc(ln1_ve, 1)
            dve.wait_ge(gate_ok, 1)
            dve.tensor_scalar(vsc[:, :], indT[:, :], gates[0:KEYS, 2:3], SC_VW, ALU.mult, ALU.mult)\
                .then_inc(vsc_ok, 1)
            dve.wait_ge(vsc_ok, 1)
            for n in of_kind["a"]:
                evacuate(n)
            for t in range(T):
                dve.wait_ge(ln1_rs, 1 + t // (T // 2))
                dve.tensor_scalar(xn[:, t, :], xall[:, t, :], mv[:, t, 0:1], rstd1[:, t:t + 1],
                                  ALU.subtract, ALU.mult).then_inc(ln1_xn, 1)
            for n in range(of_kind["x"][0], len(fills)):
                evacuate(n)
            pad = HK - (KC - 1) * P
            assert pad // 32 * 32 <= pad
            dve.wait_ge(ln1_xn, T)
            for r in range(2):
                dve.memset(probs[:, r, HK:HKP], 0.0).then_inc(ids_ok, 1)
            for b in range(B):
                dve.wait_ge(vw_ld[b], 32)
                dve.wait_ge(vw_hi, b + 1)
                dve.tensor_tensor(vwl[:, b, :, :], vwp[b], vwh[:, b, :, :], ALU.subtract).then_inc(vw_lo, 1)

            def body(s, par):
                if has(s, 5):
                    t = s - 5
                    dve.wait_ge(s_ro, t + 1)
                    dve.tensor_tensor(sc8[:, :], RS, br_b[:, :], ALU.add).then_inc(s_sb, 1)
                    wait_apart(dve, s_sb, t + 1)
                    dve.max(top8[:, :], sc8[:, :]).then_inc(s_tp, 1)
                    wait_apart(dve, s_tp, t + 1)
                    dve.max_index(idx8[:, :], top8[:, :], sc8[:, :]).then_inc(s_ix, 1)
                    dve.wait_ge(s_ix, t + 1)
                    dve.tensor_copy(idxf[:, :], idx8[:, 0:1]).then_inc(s_if, 1)
                    dve.wait_ge(s_if, t + 1)
                    dve.tensor_scalar(onehot[:, :], iota8[:, :], idxf[:, 0:1], None, ALU.is_equal)\
                        .then_inc(s_oh, 1)
                if has(s, 4):
                    t = s - 4
                    dve.wait_ge(s_pv, t + 1)
                    dve.wait_ge(ld_xr[par], (t - par) * 8 + 16)
                    wait(dve, sct[par], (t - par) * 8)
                    dve.scalar_tensor_tensor(row[:, par, 0:D], O[:, 0:D], 1.0 / (SC_P * SC_VW), xr[:, par, :],
                                             ALU.mult, ALU.add).then_inc(s_x2, 1)
                    dve.tensor_scalar(row[:, par, D + 2:D + 3], row[:, par, D + 2:D + 3], float(P), None,
                                      ALU.add).then_inc(ids_ok, 1)
                    dve.wait_ge(s_x2, t + 1)
                    dve.bn_stats(bst[:, :], row[:, par, 0:D]).then_inc(s_bs, 1)
                    wait_apart(dve, s_bs, t + 1)
                    dve.bn_aggr(mv2[:, :], bst[:, :]).then_inc(s_ag, 1)
                    dve.wait_ge(s_ag, t + 1)
                    dve.tensor_scalar(ve2[:, :], mv2[:, 1:2], EPS, None, ALU.add).then_inc(s_ve, 1)
                if has(s, 0):
                    for g, (h0, nh) in enumerate(BANKS):
                        dve.wait_ge(s_sc, NB * s + g + 1)
                        ins = dve.tensor_reduce(mx[:, h0:h0 + nh],
                                                S[g][:, 0:nh * KEYS].rearrange("p (h k) -> p h k", k=KEYS),
                                                X_AXIS, ALU.max)
                    ins.then_inc(s_mx, 1)
                    dve.wait_ge(s_mx, s + 1)
                    dve.tensor_scalar(nb[:, :], mx[:, :], -1.0 / SC_A, None, ALU.mult).then_inc(s_nb, 1)
                if has(s, 4):
                    t = s - 4
                    dve.wait_ge(s_rs, t + 1)
                    dve.scalar_tensor_tensor(row[:, par, D + 1:D + 2], mv2[:, 0:1], -1.0, row[:, par, D:D + 1],
                                             ALU.mult, ALU.mult).then_inc(s_nr, 1)
                    wait(dve, s_t2, t)
                    dve.wait_ge(s_nr, t + 1)
                    dve.tensor_scalar(xn2[:, :], row[:, par, 0:D], row[:, par, D:D + 1], row[:, par, D + 1:D + 2],
                                      ALU.mult, ALU.add).then_inc(s_xn, 1)
                if has(s, 5):
                    t = s - 5
                    dve.wait_ge(s_px, t + 1)
                    dve.tensor_tensor_reduce(junk8[:, :], onehot[:, :], RP, 1.0, 0.0, ALU.mult, ALU.add,
                                             rank[:, :]).then_inc(s_rk, 1)
                    dve.tensor_tensor(seen[:, :], seen[:, :], onehot[:, :], ALU.add).then_inc(s_ct, 1)
                    dve.wait_ge(s_rk, t + 1)
                    dve.scalar_tensor_tensor(pos[:, 1 - par, :], idxf[:, :], float(CAP), rank[:, :],
                                             ALU.mult, ALU.add).then_inc(s_po, 1)
                if has(s, 1):
                    t = s - 1
                    dve.wait_ge(s_ex, NB * (t + 1))
                    dve.reciprocal(rz[:, 1 - par, :], z[:, 1 - par, :]).then_inc(s_rz, 1)
                if has(s, 2):
                    t = s - 2
                    for g, (c0, n) in enumerate(PTB):
                        dve.wait_ge(s_ph, NB * t + g + 1)
                        dve.scalar_tensor_tensor(ptl[:, par, c0:c0 + n, :].rearrange("p c m -> p (c m)"),
                                                 PT[g][:, 0:n * P], SC_P,
                                                 pth[:, par, c0:c0 + n, :].rearrange("p c m -> p (c m)"),
                                                 ALU.mult, ALU.subtract).then_inc(s_pl, 1)
                if has_piece(s):
                    p = s - WLAG
                    dve.wait_ge(s_wh, p + 1)
                    a = (p - par) * (EXP // 2) + par * 2 * WE
                    dve.scalar_tensor_tensor(wflat[:, bass.ds(a + WE, WE)], stage[:, par, :],
                                             (SC_W1, SC_W2)[par], wflat[:, bass.ds(a, WE)],
                                             ALU.mult, ALU.subtract).then_inc(s_wl, 1)
            steps(dve, body)

            tabn = [0]

            def link(ins):
                tabn[0] += 1
                ins.then_inc(tab, 1)
                dve.wait_ge(tab, tabn[0])
            dve.wait_ge(n_ok, 1)
            v = lambda t, a, b: t[:, 0:a * b].rearrange("p (a b) -> p a b", a=a)
            link(dve.tensor_tensor(v(tA, NE, T), RP.unsqueeze(2).to_broadcast([P, NE, T]), k128[:, :, :],
                                   ALU.is_gt))
            dve.tensor_tensor(ptab[:, :], RP, ecap[:, :], ALU.add)
            link(dve.tensor_reduce(nt_e[:, :], v(tA, NE, T), X_AXIS, ALU.add))
            link(dve.tensor_tensor(v(tA, NE, NE), nt_e[:, :].unsqueeze(1).to_broadcast([P, NE, NE]),
                                   incl[:, :, :], ALU.mult))
            link(dve.tensor_reduce(cum_e[:, :], v(tA, NE, NE), X_AXIS, ALU.add))
            link(dve.tensor_tensor(v(tA, NT, NE), cum_e[:, :].unsqueeze(1).to_broadcast([P, NT, NE]),
                                   jrow[:, :, :], ALU.is_le))
            dve.tensor_reduce(ej[:, :], v(tA, NT, NE), X_AXIS, ALU.add)
            link(dve.tensor_tensor(v(tB, NT, NE), v(tA, NT, NE),
                                   nt_e[:, :].unsqueeze(1).to_broadcast([P, NT, NE]), ALU.mult))
            link(dve.tensor_reduce(sj[:, :], v(tB, NT, NE), X_AXIS, ALU.add))
            dve.tensor_scalar(vj[:, :], ej[:, :], float(NE), float(P), ALU.is_lt, ALU.mult)
            link(dve.tensor_tensor(kj[:, :], jrow[:, :, 0], sj[:, :], ALU.subtract))
            link(dve.tensor_tensor(kj[:, :], kj[:, :], vj[:, :], ALU.mult))
            dve.tensor_scalar(etab[:, :], ej[:, :], float(NE - 1), None, ALU.min)
            link(dve.scalar_tensor_tensor(rtab[:, :], ej[:, :], float(CAP), kj[:, :], ALU.mult, ALU.add))
            dve.memset(junk8[:, 0:1], 0.0).then_inc(tabs_ok, 1)

            def fbody(s, par):
                if fhas(s, 0):
                    wait(dve, f_xt, s - 1)
                    dve.wait_ge(ld_ra[par], (s - par) * 8 + 16)
                    dve.tensor_scalar(xnf[:, par, :], ra[:, par, 0:D], ra[:, par, D:D + 1], ra[:, par, D + 1:D + 2],
                                      ALU.mult, ALU.add).then_inc(f_xn, 1)
                if fhas(s, 4):
                    t = s - 4
                    e = dve.value_load(etab[0:1, bass.ds(t, 1)], min_val=0, max_val=NE - 1)
                    dve.wait_ge(f_y, t + 1)
                    if isinstance(s, int) and t == 0:
                        dve.wait_ge(ld_b2, 16)
                    wait(dve, f_yo, t)
                    dve.scalar_tensor_tensor(yt[:, :], ps[6 + par][:, 0:D], 1.0 / SC_W2,
                                             b2t[:, :, :].rearrange("p e d -> p (e d)")[:, bass.ds(e * D, D)],
                                             ALU.mult, ALU.add).then_inc(f_t1, 1)
                    dve.wait_ge(ld_rb[par], (t - par) * 8 + 16)
                    wait(dve, f_sc[par], (t - par) * 8)
                    dve.tensor_copy(ids[:, par, :], rb[:, par, D + 2:D + 3]).then_inc(f_id, 1)
                    dve.wait_ge(f_t1, t + 1)
                    dve.scalar_tensor_tensor(yo[:, par, :], yt[:, :], gates[:, 3:4], rb[:, par, 0:D],
                                             ALU.mult, ALU.add).then_inc(f_yo, 1)
                if fhas(s, 1):
                    t = s - 1
                    dve.wait_ge(f_xh, t + 1)
                    dve.tensor_tensor(fxl[:, 1 - par, :, :].rearrange("p k m -> p (k m)"), ps[1 - par][:, 0:D],
                                      fxh[:, 1 - par, :, :].rearrange("p k m -> p (k m)"),
                                      ALU.subtract).then_inc(f_xl, 1)
                if fhas(s, 2):
                    t = s - 2
                    dve.wait_ge(f_ge, 2 * (t + 1))
                    wait(dve, f_y, t - 1)
                    dve.tensor_copy(hh[:, par, :, :], hid[:, par, :, :]).then_inc(f_hh, 1)
            fsteps(dve, fbody)


_INS = ['x', 'ctx_1024', 'fside_BxS2_0', 'g_xattn', 'g_ffn', 'L0_xattn_Wq', 'L0_xattn_Wk', 'L0_xattn_Wv',
        'L0_xattn_Wo', 'L0_ffn_wr', 'L0_ffn_br', 'L0_ffn_w1', 'L0_ffn_b1', 'L0_ffn_w2', 'L0_ffn_b2']
_OUTS = [((2, 1024, 256), 'float32')]


def kernel(**inputs):
    import numpy as _np
    import concourse.bacc as _bacc
    from concourse import mybir as _mybir
    from concourse.bass_utils import run_bass_kernel_spmd as _run

    nc = _bacc.Bacc("TRN2", target_bir_lowering=False, num_devices=1)
    arrays, args = {}, []
    for name in _INS:
        a = _np.ascontiguousarray(inputs[name])
        arrays[f"in_{name}_dram"] = a
        args.append(nc.dram_tensor(f"in_{name}_dram", a.shape, _mybir.dt.from_np(a.dtype), kind="ExternalInput").ap())
    for i, (shape, dtype) in enumerate(_OUTS):
        dt = _mybir.dt.from_np(_np.dtype(dtype))
        args.append(nc.dram_tensor(f"out_{i}_dram", shape, dt, kind="ExternalOutput").ap())
    gated_cross_attention_then_routed_ffn(nc, *args)
    r = _run(nc, [arrays], core_ids=[0])
    got = tuple(r.results[0][f"out_{i}_dram"] for i in range(len(_OUTS)))
    return got[0]
```

```python
import concourse.bass as bass
from concourse import mybir
from contextlib import ExitStack

F32 = mybir.dt.float32
F16 = mybir.dt.float16
BF16 = mybir.dt.bfloat16
I32 = mybir.dt.int32
U32 = mybir.dt.uint32
ALU = mybir.AluOpType
ACT = mybir.ActivationFunctionType
X_AXIS = mybir.AxisListType.X

P = 128
EPS = 1e-5


def gated_cross_attention_then_routed_ffn(nc, x, ctx_in, ind, g_attn, g_ffn, wq, wk, wv, wo,
                                          wr, br, w1, b1, w2, b2, out):
    B, NQ, D = x.shape
    KEYS = ctx_in.shape[1]
    HD = 64
    H = wq.shape[1] // HD
    NE, _, F = w1.shape
    DK = D // P
    FC = F // P
    PAIRS = H // 2
    HK = H * KEYS
    KC = -(-HK // P)
    HKP = KC * P
    T = B * NQ // P
    assert B == 2 and D == 256 and T == 16 and F == 1024 and NE == 8
    HPB = 512 // KEYS
    BANKS = [(h0, min(HPB, H - h0)) for h0 in range(0, H, HPB)]
    NB = len(BANKS)
    PPB = HPB // 2
    SC_A = 64.0
    SC_P = 1024.0
    SC_VW = 16.0
    SC_W1 = 64.0
    SC_W2 = 256.0
    NTOK = B * NQ
    CAP = NTOK + P
    NT = (NTOK + NE * (P - 1)) // P
    ROWS = 4
    RW = D + 4
    PAD_ID = 4095.0
    rowbuf = nc.dram_tensor("rowbuf", (NE * CAP + P, RW), F32, kind="Internal").ap()
    vwbuf = nc.dram_tensor("vwbuf", (B, HK, D), F32, kind="Internal").ap()
    outf = out.rearrange("b n d -> (b n) d")

    FLAG = 5
    ctx = ExitStack()
    with ctx:
        def sb(name, shape, dt):
            return ctx.enter_context(nc.sbuf_tensor(name, shape, dt))

        def sem(name):
            return ctx.enter_context(nc.semaphore(name))

        WE = 2 * F
        WALL = sb("WALL", [P, NE, 4, WE], F16)
        wflat = WALL[:, :, :, :].rearrange("p e q n -> p (e q n)")
        EXP = 4 * WE

        def early(expert, n, off=0):
            a = expert * EXP + 2 * off
            return wflat[:, a:a + 2 * n].bitcast(F32)
        kbd = early(0, PAIRS * B * 2 * KEYS).rearrange("p (a b j k) -> p a b j k", a=PAIRS, b=B, j=2)
        vbd = early(0, PAIRS * B * 2 * KEYS, PAIRS * B * 2 * KEYS)\
            .rearrange("p (a b j k) -> p a b j k", a=PAIRS, b=B, j=2)
        bd_all = early(0, 2 * PAIRS * B * 2 * KEYS)
        wqT = early(0, PAIRS * D, 2 * PAIRS * B * 2 * KEYS).rearrange("p (a d) -> p a d", a=PAIRS)
        used = 2 * PAIRS * B * 2 * KEYS + PAIRS * D
        ctx_s = early(0, B * D, used)[0:KEYS, :].rearrange("p (b d) -> p b d", b=B)
        ctxT = early(0, DK * B * KEYS, used + B * D).rearrange("p (k m) -> p k m", k=DK)
        assert 2 * (used + B * D + DK * B * KEYS) <= 2 * EXP
        xn = early(2, T * D).rearrange("p (t d) -> p t d", t=T)
        xall = early(3, T * D).rearrange("p (t d) -> p t d", t=T)
        vwp = [early(3, KC * D).rearrange("p (c d) -> p c d", c=KC),
               early(2, KC * D).rearrange("p (c d) -> p c d", c=KC)]
        wk_s = early(4, DK * H * HD).rearrange("p (k n) -> p k n", k=DK)
        wv_s = early(4, DK * H * HD, DK * H * HD).rearrange("p (k n) -> p k n", k=DK)
        wq_s = early(5, DK * H * HD).rearrange("p (k n) -> p k n", k=DK)
        wo_s = early(5, PAIRS * D, PAIRS * D).rearrange("p (a d) -> p a d", a=PAIRS)
        A0 = 6 * EXP
        ah = wflat[:, A0:A0 + B * DK * HK].rearrange("p (b k n) -> p b k n", b=B, k=DK)
        al = wflat[:, A0 + B * DK * HK:A0 + 2 * B * DK * HK].rearrange("p (b k n) -> p b k n", b=B, k=DK)
        E0 = A0 + 2 * B * DK * HK
        probs = wflat[:, E0:E0 + 4 * HKP].bitcast(F32).rearrange("p (r n) -> p r n", r=2)
        assert E0 + 4 * HKP <= NE * EXP

        stage = sb("stage", [P, 2, WE], F32)
        vwf = stage[0:KEYS, :, :].rearrange("p r (h d) -> p r h d", d=D)
        row = sb("row", [P, ROWS, RW], F32)
        ident = sb("ident", [P, P], F32)
        upper = sb("upper", [P, P], BF16)
        ones = sb("ones", [P, P], BF16)
        wr_s = sb("wr_s", [P, DK, NE], F32)
        br_b = sb("br_b", [P, NE], F32)
        b1r = sb("b1r", [NE * FC, P], F32)
        b1c = sb("b1c", [P, NE * FC], F32)
        gates = sb("gates", [P, 4], F32)
        indT = sb("indT", [KEYS, B], F32)
        vsc = sb("vsc", [KEYS, B], F32)
        mv = sb("mv", [P, T, 2], F32)
        rstd1 = sb("rstd1", [P, T], F32)
        nhalf = sb("nhalf", [P, T], F32)
        bst = sb("bst", [P, 6], F32)
        mv2 = sb("mv2", [P, 2], F32)
        ve2 = sb("ve2", [P, 1], F32)
        mx = sb("mx", [P, H], F32)
        nb = sb("nb", [P, H], F32)
        z = sb("z", [P, 2, H], F32)
        rz = sb("rz", [P, 2, H], F32)
        sc8 = sb("sc8", [P, NE], F32)
        top8 = sb("top8", [P, NE], F32)
        idx8 = sb("idx8", [P, NE], U32)
        idxf = sb("idxf", [P, 1], F32)
        iota8 = sb("iota8", [P, NE], F32)
        onehot = sb("onehot", [P, NE], BF16)
        seen = sb("seen", [P, NE], BF16)
        junk8 = sb("junk8", [P, NE], F32)
        rank = sb("rank", [P, 1], F32)
        pos = sb("pos", [P, ROWS, 1], I32)
        ids = sb("ids", [P, 2, 1], I32)
        k128 = sb("k128", [P, NE, T], F32)
        incl = sb("incl", [P, NE, NE], F32)
        jrow = sb("jrow", [P, NT, NE], F32)
        ecap = sb("ecap", [P, NE], F32)
        tA = sb("tA", [P, NT * NE], F32)
        tB = sb("tB", [P, NT * NE], F32)
        nt_e = sb("nt_e", [P, NE], F32)
        cum_e = sb("cum_e", [P, NE], F32)
        ej = sb("ej", [P, NT], F32)
        sj = sb("sj", [P, NT], F32)
        kj = sb("kj", [P, NT], F32)
        vj = sb("vj", [P, NT], F32)
        etab = sb("etab", [P, NT], I32)
        rtab = sb("rtab", [P, NT], I32)
        ptab = sb("ptab", [P, NE], I32)
        QP = (NT + FLAG + 1) // 2
        epad = sb("epad", [P, 2 * QP + 4], F32)
        qacc = sb("qacc", [P, 2, QP], F32)
        qtab = sb("qtab", [P, QP], I32)
        sc1 = ctx.enter_context(nc.sbuf_tensor("padrow", [P, RW], F32))

        inner = ExitStack()

        def sbi(name, shape, dt):
            return inner.enter_context(nc.sbuf_tensor(name, shape, dt))
        xth = sbi("xth", [P, DK, T * P], F16)
        xtl = sbi("xtl", [P, DK, T * P], F16)
        vwh = sbi("vwh", [P, B, KC, D], F16)
        vwl = sbi("vwl", [P, B, KC, D], F16)
        pth = sbi("pth", [P, 2, KC, P], F16)
        ptl = sbi("ptl", [P, 2, KC, P], F16)
        xr = sbi("xr", [P, 2, D], F32)
        xn2 = sbi("xn2", [P, D], F32)
        xt2 = sbi("xt2", [P, DK, P], F32)
        inner.close()
        inner = ExitStack()
        b2t = sbi("b2t", [P, NE, D], F32)
        ra = sbi("ra", [P, 2, RW], F32)
        rb = sbi("rb", [P, 2, RW], F32)
        xnf = sbi("xnf", [P, 2, D], F32)
        fxh = sbi("fxh", [P, 2, DK, P], F16)
        fxl = sbi("fxl", [P, 2, DK, P], F16)
        hid = sbi("hid", [P, 2, FC, P], F32)
        hh = sbi("hh", [P, 2, FC, P], F16)
        hl = sbi("hl", [P, 2, FC, P], F16)
        yt = sbi("yt", [P, D], F32)
        yo = sbi("yo", [P, 2, D], F32)
        inner.close()

        ps = [ctx.enter_context(nc.psum_tensor(f"ps{i}", [P, 512], F32)) for i in range(8)]
        S = ps[0:NB]
        PT = ps[3:6]
        O = ps[6]
        R = ps[7]
        RT, RS, RP = R[:, 0:D], R[:, D:D + NE], O[:, D:D + NE]
        CPB = 4
        PTB = [(c0, min(CPB, KC - c0)) for c0 in range(0, KC, CPB)]

        ld_ctx, ld_wk, ld_wv, ld_wq, ld_wo = (sem(n) for n in ("ld_ctx", "ld_wk", "ld_wv", "ld_wq", "ld_wo"))
        ld_x = [sem("ld_x0"), sem("ld_x1")]
        ld_small = sem("ld_small")
        ld_b1 = sem("ld_b1")
        consts = sem("consts")
        passed = sem("passed")
        const_id = sem("const_id")
        bd_zero = sem("bd_zero")
        filled = sem("filled")
        act_out = sem("act_out")
        dve_out = sem("dve_out")
        gate_ok = sem("gate_ok")
        vsc_ok = sem("vsc_ok")
        ln1_st = sem("ln1_st")
        ln1_mv = sem("ln1_mv")
        ln1_ve = sem("ln1_ve")
        ln1_rs = sem("ln1_rs")
        ln1_xn = sem("ln1_xn")
        vw_st = [sem("vw_st0"), sem("vw_st1")]
        vw_ld = [sem("vw_ld0"), sem("vw_ld1")]
        vw_hi = sem("vw_hi")
        vw_lo = sem("vw_lo")
        s_sc = sem("s_sc")
        s_mx = sem("s_mx")
        s_nb = sem("s_nb")
        s_ex = sem("s_ex")
        ids_ok = sem("ids_ok")
        ids_set = sem("ids_set")
        s_rz = sem("s_rz")
        s_nm = sem("s_nm")
        s_pt = sem("s_pt")
        s_ph = sem("s_ph")
        s_pl = sem("s_pl")
        s_pv = sem("s_pv")
        s_x2 = sem("s_x2")
        s_bs = sem("s_bs")
        s_ag = sem("s_ag")
        s_ve = sem("s_ve")
        s_rs = sem("s_rs")
        s_nr = sem("s_nr")
        s_xn = sem("s_xn")
        s_t2 = sem("s_t2")
        s_tc = sem("s_tc")
        s_ro = sem("s_ro")
        s_sb = sem("s_sb")
        s_tp = sem("s_tp")
        s_ix = sem("s_ix")
        s_if = sem("s_if")
        s_oh = sem("s_oh")
        s_px = sem("s_px")
        s_rk = sem("s_rk")
        s_po = sem("s_po")
        s_ct = sem("s_ct")
        row_free = [sem(f"row_free{r}") for r in range(ROWS)]
        ld_xr = [sem("ld_xr0"), sem("ld_xr1")]
        ld_st = [sem("ld_st0"), sem("ld_st1")]
        s_wh = sem("s_wh")
        s_wl = sem("s_wl")
        pad0 = sem("pad0")
        padded = sem("padded")
        ld_b2 = sem("ld_b2")
        tab = sem("tab")
        tabs_ok = sem("tabs_ok")
        n_ok = sem("n_ok")
        ld_ra = [sem("ld_ra0"), sem("ld_ra1")]
        ld_rb = [sem("ld_rb0"), sem("ld_rb1")]
        f_xn = sem("f_xn")
        f_xt = sem("f_xt")
        f_xh = sem("f_xh")
        f_xl = sem("f_xl")
        f_h = sem("f_h")
        f_ge = sem("f_ge")
        f_hh = sem("f_hh")
        f_hl = sem("f_hl")
        f_y = sem("f_y")
        f_t1 = sem("f_t1")
        f_yo = sem("f_yo")
        f_id = sem("f_id")
        f_sc = [sem("f_sc0"), sem("f_sc1")]

        block = ctx.enter_context(nc.Block())

        NCONSTS = 12

        def wait(eng, s, v):
            if not isinstance(v, int) or v > 0:
                eng.wait_ge(s, v)

        def wait_apart(eng, s, v):
            wait(eng, s, v)
            eng.sem_inc(passed, 1)

        LAG = 4
        PEEL = 8
        def steps(eng, body):
            for s in range(PEEL):
                body(s, s % ROWS)
            with eng.Fori(PEEL // ROWS, T // ROWS) as q:
                for r in range(ROWS):
                    body(ROWS * q + r, r)
            for s in range(T, T + LAG):
                body(s, s % ROWS)

        def has(s, lag):
            return not isinstance(s, int) or 0 <= s - lag < T

        FPEEL = 8

        def fsteps(eng, body):
            for s in range(FPEEL):
                body(s, s % 2)
            with eng.Fori(FPEEL // 2, NT // 2) as q:
                body(2 * q, 0)
                body(2 * q + 1, 1)
            for s in range(NT - NT % 2, NT + FLAG):
                body(s, s % 2)

        def fhas(s, lag):
            return not isinstance(s, int) or 0 <= s - lag < NT

        WLAG = 3
        NP = 2 * NE

        def has_piece(s):
            return not isinstance(s, int) or 0 <= s - WLAG < NP

        fills = [("ctxT", 0, "D")]
        fills += [("k", g, "D") for g in range(NB)]
        fills += [("wqT", g, "AD"[g % 2]) for g in range(4)]
        fills += [("b1", 0, "D")]
        fills += [("a", (b, k, g), "D") for b in range(B) for k in range(DK) for g in range(NB)]
        fills += [("x", g, "D") for g in range(T // 2)]
        fills += [("v", g, "D") for g in range(NB)]
        fills += [("vw", (b, i), "AD"[i % 2]) for b in range(B) for i in range(PAIRS)]
        released = []
        n_rel = {"A": 0, "D": 0}
        for kind, _, who in fills:
            n_rel[who] += 1
            released.append((who, n_rel[who]))
        hi_done = sem("hi_done")
        his = {}
        for n, (kind, _, _) in enumerate(fills):
            if kind in ("a", "x"):
                his[n] = len(his) + 1
        of_kind = {}
        for n, (kind, arg, _) in enumerate(fills):
            of_kind.setdefault(kind, []).append(n)

        def emptied(eng, n):
            who, v = released[n]
            eng.wait_ge(act_out if who == "A" else dve_out, v)

        def all_emptied(eng, kind):
            for who in "AD":
                v = max([released[n][1] for n in of_kind[kind] if released[n][0] == who], default=0)
                if v:
                    eng.wait_ge(act_out if who == "A" else dve_out, v)

        @block.sync
        def _(sp):
            sp.dma_start(ctx_s[:, :, :], ctx_in.rearrange("b k d -> k b d")).then_inc(ld_ctx, 16)
            sp.dma_start(wk_s, wk.rearrange("(k p) n -> p k n", p=P)).then_inc(ld_wk, 16)
            xv = x.rearrange("b (n p) d -> p n b d", p=P)
            xa = xall.rearrange("p (n b) d -> p n b d", b=B)
            sp.dma_start(wq_s, wq.rearrange("(k p) n -> p k n", p=P)).then_inc(ld_wq, 16)
            for i in range(2):
                for b in range(B):
                    sp.dma_start(xa[:, i * T // 4:(i + 1) * T // 4, b, :],
                                 xv[:, i * T // 4:(i + 1) * T // 4, b, :]).then_inc(ld_x[i], 16)
            sp.dma_start(wv_s, wv.rearrange("(k p) n -> p k n", p=P)).then_inc(ld_wv, 16)
            sp.dma_start(wo_s, wo.rearrange("(a p) d -> p a d", p=P)).then_inc(ld_wo, 16)
            vws = [vwbuf[b].rearrange("(h k) d -> k h d", h=H) for b in range(B)]
            vwn = of_kind["vw"]
            for b in range(B):
                for half in range(2):
                    last = vwn[b * PAIRS + half * PAIRS // 2 + PAIRS // 2 - 1]
                    emptied(sp, last)
                    emptied(sp, last - 1)
                    sp.dma_start(vws[b][:, half * H // 2:(half + 1) * H // 2, :],
                                 vwf[:, half, :, :]).then_inc(vw_st[half], 16)
            for b in range(B):
                for half in range(2):
                    sp.wait_ge(vw_st[half], 16 * (b + 1))
                full = HK // P
                all_emptied(sp, "x")
                sp.dma_start(vwp[b][:, 0:full, :],
                             vwbuf[b, 0:full * P, :].rearrange("(c p) d -> p c d", p=P)).then_inc(vw_ld[b], 16)
                sp.dma_start(vwp[b][0:HK - full * P, full, :], vwbuf[b, full * P:HK, :]).then_inc(vw_ld[b], 16)

            def body(s, quad):
                par = quad % 2
                if has_piece(s + 1):
                    p = s + 1 - WLAG
                    pp = par
                    wait(sp, s_wh, p - 1)
                    wait(sp, s_wl, p - 1)
                    if isinstance(s, int):
                        w1e, w2e = w1[p // 2], w2[p // 2]
                    else:
                        w1e = w1.rearrange("e d f -> (e d) f")[bass.ds((p - pp) * (D // 2), D), :]
                        w2e = w2.rearrange("e f d -> (e f) d")[bass.ds((p - pp) * (F // 2), F), :]
                    if pp == 0:
                        sp.dma_start(stage[:, 0, :].rearrange("p (k n) -> p k n", k=DK),
                                     w1e.rearrange("(k p) n -> p k n", p=P)).then_inc(ld_st[0], 16)
                    else:
                        sp.dma_start(stage[:, 1, :].rearrange("p (c d) -> p c d", c=FC),
                                     w2e.rearrange("(c p) d -> p c d", p=P)).then_inc(ld_st[1], 16)
            steps(sp, body)
            sp.wait_ge(s_pv, T)
            sp.wait_ge(s_ro, T)
            sp.dma_start(b2t[:, :, :].rearrange("p e d -> p (e d)"),
                         b2.rearrange("e d -> (e d)").unsqueeze(0).to_broadcast([P, NE * D])).then_inc(ld_b2, 16)
            sp.wait_ge(pad0, 1)
            sp.wait_ge(tabs_ok, 1)
            sp.dma_start(rowbuf[NE * CAP:NE * CAP + P, :], sc1[:, :]).then_inc(padded, 16)
            with sp.Fori(0, NE) as e:
                r = sp.value_load(ptab[0:1, bass.ds(e, 1)], min_val=0, max_val=NE * CAP)
                sp.dma_start(rowbuf[bass.ds(r, P), :], sc1[:, :]).then_inc(padded, 16)
            sp.wait_ge(padded, 16 * (NE + 1))
            for i in range(ROWS):
                sp.wait_ge(row_free[i], 16 * (T // ROWS))

            def fbody(s, par):
                if fhas(s, 0):
                    wait(sp, f_xn, s - 1)
                    r = sp.value_load(rtab[0:1, bass.ds(s, 1)], min_val=0, max_val=NE * CAP)
                    sp.dma_start(ra[:, par, :], rowbuf[bass.ds(r, P), :]).then_inc(ld_ra[par], 16)
                if fhas(s, 4):
                    t = s - 4
                    wait(sp, f_yo, t - 1)
                    wait(sp, f_id, t - 1)
                    r = sp.value_load(rtab[0:1, bass.ds(t, 1)], min_val=0, max_val=NE * CAP)
                    sp.dma_start(rb[:, par, :], rowbuf[bass.ds(r, P), :]).then_inc(ld_rb[par], 16)
            fsteps(sp, fbody)

        @block.gpsimd
        def _(pool):
            pool.memset(ident[:, :], 0.0).then_inc(const_id, 1)
            pool.memset(upper[:, :], 1.0).then_inc(const_id, 1)
            pool.memset(incl[:, :, :], 1.0).then_inc(const_id, 1)
            pool.wait_ge(const_id, 3)
            pool.affine_select(out=ident[:, :], in_=ident[:, :], compare_op=ALU.not_equal, fill=1.0,
                               base=0, pattern=[[-1, P]], channel_multiplier=1).then_inc(consts, 1)
            pool.affine_select(out=upper[:, :], in_=upper[:, :], compare_op=ALU.is_gt, fill=0.0,
                               base=0, pattern=[[1, P]], channel_multiplier=-1).then_inc(consts, 1)
            pool.affine_select(out=incl[:, :, :], in_=incl[:, :, :], compare_op=ALU.is_ge, fill=0.0,
                               base=0, pattern=[[1, NE], [-1, NE]], channel_multiplier=0).then_inc(consts, 1)
            pool.memset(ones[:, :], 1.0).then_inc(consts, 1)
            pool.memset(seen[:, :], 0.0).then_inc(consts, 1)
            pool.memset(nhalf[:, :], -0.5).then_inc(consts, 1)
            pool.memset(epad[:, :], 0.0).then_inc(consts, 1)
            iota = lambda dst, pattern, base, cm: pool.iota(
                dst, pattern, base=base, channel_multiplier=cm,
                allow_small_or_imprecise_dtypes=True).then_inc(consts, 1)
            iota(iota8[:, :], [[1, NE]], 0, 0)
            iota(k128[:, :, :], [[0, NE], [P, T]], 0, 0)
            iota(jrow[:, :, :], [[1, NT], [0, NE]], 0, 0)
            iota(ecap[:, :], [[CAP, NE]], 0, 0)
            for r in range(ROWS):
                pool.iota(row[:, r, D + 2:D + 3], [[0, 1]], base=(r % B) * NQ + (r // B - ROWS // B) * P,
                          channel_multiplier=1, allow_small_or_imprecise_dtypes=True).then_inc(ids_set, 1)
            pool.wait_ge(ids_set, ROWS)
            pool.memset(row[:, :, D + 3:D + 4], 0.0).then_inc(consts, 1)
            pool.memset(sc1[:, :], 0.0).then_inc(const_id, 1)
            pool.wait_ge(const_id, 4)
            pool.memset(sc1[:, D + 2:D + 3], PAD_ID).then_inc(pad0, 1)
            pool.wait_ge(ln1_ve, 1)
            pool.tensor_tensor(rstd1[:, 0:T // 2], rstd1[:, 0:T // 2], nhalf[:, 0:T // 2], ALU.pow)\
                .then_inc(ln1_rs, 1)
            pool.wait_ge(ln1_ve, 2)
            pool.tensor_tensor(rstd1[:, T // 2:T], rstd1[:, T // 2:T], nhalf[:, T // 2:T], ALU.pow)\
                .then_inc(ln1_rs, 1)

            def body(s, quad):
                par = quad % 2
                if has(s, 3):
                    pool.wait_ge(s_ve, s - 3 + 1)
                    pool.tensor_tensor(row[:, (quad + 1) % ROWS, D:D + 1], ve2[:, :], nhalf[:, 0:1], ALU.pow).then_inc(s_rs, 1)
                if has(s, 4):
                    wait_apart(pool, s_po, s - 4 + 1)
                    pool.indirect_dma_start(rowbuf[:, :], bass.IndirectOffsetOnAxis(pos[:, quad, :], 0),
                                            row[:, quad, :], None).then_inc(row_free[quad], 16)
                if has(s, 0):
                    pool.wait_ge(s_rz, s + 1)
                    pv = probs[:, par, 0:HK].rearrange("p (h k) -> p h k", h=H)
                    pool.tensor_tensor(pv, pv, rz[:, par, :].unsqueeze(2).to_broadcast([P, H, KEYS]),
                                       ALU.mult).then_inc(s_nm, 1)
            steps(pool, body)

            def fbody(s, par):
                if fhas(s, 2):
                    t = s - 2
                    pool.wait_ge(f_hh, t + 1)
                    wait(pool, f_y, t - 1)
                    pool.tensor_tensor(hl[:, par, :, :], hid[:, par, :, :], hh[:, par, :, :],
                                       ALU.subtract).then_inc(f_hl, 1)
                if fhas(s, 5):
                    pool.wait_ge(f_id, s - 5 + 1)
                    pool.wait_ge(f_yo, s - 5 + 1)
                    pool.sem_inc(passed, 1)
                    pool.indirect_dma_start(outf[:, :], bass.IndirectOffsetOnAxis(ids[:, 1 - par, :], 0),
                                            yo[:, 1 - par, :], None, bounds_check=NTOK - 1,
                                            oob_is_err=False).then_inc(f_sc[1 - par], 16)
            fsteps(pool, fbody)
            for i in range(2):
                pool.wait_ge(f_sc[i], 16 * ((NT + 1 - i) // 2))

        @block.scalar
        def _(act):
            act.dma_start(gates[:, 0:1], g_attn.unsqueeze(0).to_broadcast([P, 1])).then_inc(ld_small, 16)
            act.dma_start(gates[:, 1:2], g_ffn.unsqueeze(0).to_broadcast([P, 1])).then_inc(ld_small, 16)
            with nc.allow_non_contiguous_dma(reason="154 values, keys on partitions"):
                act.dma_start(indT[:, :], ind.rearrange("b k -> k b")).then_inc(ld_small, 16)
            act.dma_start(wr_s[:, :, :], wr.rearrange("(k p) e -> p k e", p=P)).then_inc(ld_small, 16)
            act.dma_start(br_b[:, :], br.unsqueeze(0).to_broadcast([P, NE])).then_inc(ld_small, 16)
            act.dma_start(b1r[:, :], b1.rearrange("e (c p) -> (e c) p", p=P)).then_inc(ld_b1, 16)
            act.wait_ge(ld_small, 80)
            act.activation(gates[:, 2:4], gates[:, 0:2], ACT.Tanh).then_inc(gate_ok, 1)
            for n, (kind, arg, who) in enumerate(fills):
                bank = ps[n % 8]
                if kind == "k" or kind == "v":
                    pass
                elif kind == "wqT" and who == "A":
                    act.wait_ge(filled, n + 1)
                    act.activation(wqT[:, 2 * arg:2 * arg + 2, :].rearrange("p a d -> p (a d)"),
                                   bank[:, :], ACT.Copy).then_inc(act_out, 1)
                elif kind == "a":
                    b, k, g = arg
                    h0, nh = BANKS[g]
                    act.wait_ge(filled, n + 1)
                    act.activation(ah[:, b, k, h0 * KEYS:(h0 + nh) * KEYS], bank[:, 0:nh * KEYS],
                                   ACT.Copy, scale=SC_A / HD ** 0.5).then_inc(hi_done, 1)
                elif kind == "x":
                    act.wait_ge(filled, n + 1)
                    act.activation(xth[:, :, 2 * arg * P:(2 * arg + 2) * P],
                                   bank[:, :].rearrange("p (k m) -> p k m", k=DK), ACT.Copy).then_inc(hi_done, 1)
                elif kind == "vw" and who == "A":
                    b, i = arg
                    half = i // (PAIRS // 2)
                    if b:
                        act.wait_ge(vw_st[half], 16 * b)
                    act.wait_ge(filled, n + 1)
                    act.wait_ge(vsc_ok, 1)
                    j = 2 * (i % (PAIRS // 2))
                    act.activation(vwf[:, half, j:j + 2, :].rearrange("p h d -> p (h d)"), bank[0:KEYS, :],
                                   ACT.Copy, scale=vsc[:, b:b + 1]).then_inc(act_out, 1)
            for b in range(B):
                act.wait_ge(vw_ld[b], 32)
                act.activation(vwh[:, b, :, :], vwp[b], ACT.Copy).then_inc(vw_hi, 1)

            def body(s, quad):
                par = quad % 2
                if has(s, 0):
                    wait(act, s_pt, NB * (s - 1))
                    wait(act, s_rz, s - 1)
                    for g, (h0, nh) in enumerate(BANKS):
                        act.wait_ge(s_nb, NB * s + g + 1)
                        for h in range(h0, h0 + nh):
                            ins = act.activation(probs[:, par, h * KEYS:(h + 1) * KEYS],
                                                 S[g][:, (h - h0) * KEYS:(h - h0 + 1) * KEYS], ACT.Exp,
                                                 bias=nb[:, h:h + 1], scale=1.0 / SC_A,
                                                 accum_out=z[:, par, h:h + 1])
                        ins.then_inc(s_ex, 1)
                if has(s, 2):
                    t = s - 2
                    wait(act, s_x2, t - 1)
                    bt = par
                    if isinstance(s, int):
                        src = x[bt, (t // 2) * P:(t // 2 + 1) * P, :]
                    else:
                        src = x[bt, bass.ds((t - bt) * (P // 2), P), :]
                    act.dma_start(xr[:, par, :], src).then_inc(ld_xr[par], 16)
                if has(s, 1):
                    t = s - 1
                    wait(act, s_pv, t - 1)
                    for g, (c0, n) in enumerate(PTB):
                        act.wait_ge(s_pt, NB * t + g + 1)
                        act.activation(pth[:, 1 - par, c0:c0 + n, :].rearrange("p c m -> p (c m)"),
                                       PT[g][:, 0:n * P], ACT.Copy, scale=SC_P).then_inc(s_ph, 1)
                if has_piece(s):
                    p, pp = s - WLAG, 1 - par
                    if isinstance(s, int) and s >= T:
                        act.wait_ge(s_sc, NB * T)
                        act.wait_ge(s_pt, NB * T)
                    act.wait_ge(ld_st[pp], 16 * ((p - pp) // 2 + 1) if isinstance(s, int)
                                else (p - pp) * 8 + 16)
                    dst = wflat[:, bass.ds((p - pp) * (EXP // 2) + pp * 2 * WE, WE)]
                    act.activation(dst, stage[:, pp, :], ACT.Copy, scale=(SC_W1, SC_W2)[pp]).then_inc(s_wh, 1)
                if has(s, 3):
                    act.wait_ge(s_t2, s - 3 + 1)
                    wait(act, s_ro, s - 3)
                    act.activation(xt2[:, :, :].rearrange("p k m -> p (k m)"), RT, ACT.Copy).then_inc(s_tc, 1)
            steps(act, body)

            def fbody(s, par):
                if fhas(s, 1):
                    t = s - 1
                    act.wait_ge(f_xt, t + 1)
                    wait(act, f_h, 2 * (t - 1))
                    act.activation(fxh[:, 1 - par, :, :].rearrange("p k m -> p (k m)"), ps[1 - par][:, 0:D],
                                   ACT.Copy).then_inc(f_xh, 1)
                if fhas(s, 2):
                    t = s - 2
                    e = act.value_load(etab[0:1, bass.ds(t, 1)], min_val=0, max_val=NE - 1)
                    wait(act, f_hl, t - 1)
                    for g in range(2):
                        act.wait_ge(f_h, 2 * t + g + 1)
                        for c in range(FC // 2):
                            cc = g * FC // 2 + c
                            ins = act.activation(hid[:, par, cc, :], ps[2 + 2 * par + g][:, c * P:(c + 1) * P],
                                                 ACT.Gelu, bias=b1c[:, bass.ds(e * FC + cc, 1)],
                                                 scale=1.0 / SC_W1)
                        ins.then_inc(f_ge, 1)
            fsteps(act, fbody)

        @block.tensor
        def _(pe):
            pe.wait_ge(consts, NCONSTS)
            for n, (kind, arg, who) in enumerate(fills):
                bank = ps[n % 8]
                if n >= 8:
                    emptied(pe, n - 8)
                if kind == "ctxT":
                    pe.wait_ge(ld_ctx, 16)
                    for k in range(DK):
                        for b in range(B):
                            c = (k * B + b) * KEYS
                            ins = pe.transpose(bank[:, c:c + KEYS], ctx_s[:, b, k * P:(k + 1) * P],
                                               ident[0:KEYS, 0:KEYS])
                elif kind in "kv":
                    if arg == 0:
                        emptied(pe, of_kind["ctxT"][0])
                        pe.wait_ge(ld_wk if kind == "k" else ld_wv, 16)
                    w = wk_s if kind == "k" else wv_s
                    pairs = range(arg * PPB, min((arg + 1) * PPB, PAIRS))
                    for i, a in enumerate(pairs):
                        for k in range(DK):
                            ins = pe.matmul(bank[:, i * B * KEYS:(i + 1) * B * KEYS],
                                            w[:, k, a * P:(a + 1) * P], ctxT[:, k, :],
                                            start=(k == 0), stop=(k == DK - 1))
                elif kind == "wqT":
                    if arg == 0:
                        pe.wait_ge(ld_wq, 16)
                    for i in range(2):
                        for k in range(DK):
                            a = 2 * arg + i
                            ins = pe.transpose(bank[:, (i * DK + k) * P:(i * DK + k + 1) * P],
                                               wq_s[:, k, a * P:(a + 1) * P], ident[:, :])
                elif kind == "b1":
                    pe.wait_ge(ld_b1, 16)
                    ins = pe.transpose(bank[:, 0:NE * FC], b1r[:, :], ident[0:NE * FC, 0:NE * FC])
                elif kind == "a":
                    b, k, g = arg
                    if n == of_kind["a"][0]:
                        all_emptied(pe, "wqT")
                        all_emptied(pe, "k")
                    for i, a in enumerate(range(g * PPB, min((g + 1) * PPB, PAIRS))):
                        ins = pe.matmul(bank[:, i * 2 * KEYS:(i + 1) * 2 * KEYS], wqT[:, a, k * P:(k + 1) * P],
                                        kbd[:, a, b, :, :].rearrange("p j k -> p (j k)"), start=True, stop=True)
                elif kind == "x":
                    pe.wait_ge(ln1_xn, 2 * arg + 2)
                    for k in range(DK):
                        for i in range(2):
                            ins = pe.transpose(bank[:, (k * 2 + i) * P:(k * 2 + i + 1) * P],
                                               xn[:, 2 * arg + i, k * P:(k + 1) * P], ident[:, :])
                elif kind == "vw":
                    b, a = arg
                    if n == of_kind["vw"][0]:
                        all_emptied(pe, "v")
                        pe.wait_ge(ld_wo, 16)
                    for j in range(2):
                        ins = pe.matmul(bank[0:KEYS, j * D:(j + 1) * D], vbd[:, a, b, j, :], wo_s[:, a, :],
                                        start=True, stop=True)
                ins.then_inc(filled, 1)
            for n in range(len(fills) - 8, len(fills)):
                emptied(pe, n)

            def router(s):
                if has(s, 4):
                    t = s - 4
                    pe.wait_ge(s_tc, t + 1)
                    for k in range(DK):
                        ins = pe.matmul(RS, xt2[:, k, :], wr_s[:, k, :], start=(k == 0), stop=(k == DK - 1))
                    ins.then_inc(s_ro, 1)

            def body(s, quad):
                par = quad % 2
                if not has(s, 0):
                    router(s)
                if has(s, 0):
                    xs = bass.ds(s * P, P)
                    for g, (h0, nh) in enumerate(BANKS):
                        if g == NB - 1:
                            router(s)
                        cols = slice(h0 * KEYS, (h0 + nh) * KEYS)
                        wait(pe, s_ex, NB * (s - 1) + g + 1)
                        for k in range(DK):
                            for i, (l, r) in enumerate(((xth, ah), (xth, al), (xtl, ah))):
                                ins = pe.matmul(S[g][:, 0:nh * KEYS], l[:, k, xs], r[:, par, k, cols],
                                                start=(k == 0 and i == 0), stop=(k == DK - 1 and i == 2))
                        ins.then_inc(s_sc, 1)
                if has(s, 1):
                    t = s - 1
                    pe.wait_ge(s_nm, t + 1)
                    for g, (c0, n) in enumerate(PTB):
                        wait(pe, s_pl, NB * (t - 1) + g + 1)
                        for i in range(n):
                            c = c0 + i
                            ins = pe.transpose(PT[g][:, i * P:(i + 1) * P], probs[:, 1 - par, c * P:(c + 1) * P],
                                               ident[:, :])
                        ins.then_inc(s_pt, 1)
                if has(s, 2):
                    t = s - 2
                    wait(pe, s_x2, t)
                    pb = par
                    for g, (c0, n) in enumerate(PTB):
                        pe.wait_ge(s_pl, NB * t + g + 1)
                        for c in range(c0, c0 + n):
                            for i, (l, r) in enumerate(((pth, vwh), (pth, vwl), (ptl, vwh))):
                                ins = pe.matmul(O[:, 0:D], l[:, pb, c, :], r[:, pb, c, :],
                                                start=(c == 0 and i == 0), stop=(c == KC - 1 and i == 2))
                    ins.then_inc(s_pv, 1)
                if has(s, 4):
                    t = s - 4
                    pe.wait_ge(s_oh, t + 1)
                    pe.matmul(RP, upper[:, :], onehot[:, :], start=True, stop=False)
                    pe.matmul(RP, ones[:, :], seen[:, :], start=False, stop=True).then_inc(s_px, 1)
                if has(s, 3):
                    t = s - 3
                    pe.wait_ge(s_xn, t + 1)
                    for k in range(DK):
                        ins = pe.transpose(R[:, k * P:(k + 1) * P], xn2[:, k * P:(k + 1) * P], ident[:, :])
                    ins.then_inc(s_t2, 1)
            steps(pe, body)
            pe.wait_ge(s_ct, T)
            pe.matmul(RP, ones[:, :], seen[:, :], start=True, stop=True).then_inc(n_ok, 1)
            pe.wait_ge(tabs_ok, 1)
            packed = [None]

            def fbody(s, par):
                if par == 0:
                    packed[0] = pe.value_load(qtab[0:1, bass.ds(s // 2, 1)], min_val=0, max_val=NE ** 4 - 1)

                def e_of(digit):
                    return packed[0] // NE ** digit % NE
                if fhas(s, 1):
                    t = s - 1
                    pe.wait_ge(f_xn, t + 1)
                    wait(pe, f_xl, t - 1)
                    for k in range(DK):
                        ins = pe.transpose(ps[1 - par][:, k * P:(k + 1) * P], xnf[:, 1 - par, k * P:(k + 1) * P],
                                           ident[:, :])
                    ins.then_inc(f_xt, 1)
                if fhas(s, 4):
                    t = s - 4
                    e_out = e_of(par)
                    pe.wait_ge(f_hl, t + 1)
                    wait(pe, f_yo, t - 1)
                if fhas(s, 2):
                    t = s - 2
                    e_in = e_of(2 + par)
                    pe.wait_ge(f_xl, t + 1)
                    wait(pe, f_ge, 2 * (t - 1))
                for c in range(FC):
                    if fhas(s, 2):
                        hb = ps[2 + 2 * par + c // (FC // 2)]
                        dst = hb[:, (c % (FC // 2)) * P:(c % (FC // 2) + 1) * P]
                        for k in range(DK):
                            for i, (q, r) in enumerate(((0, fxh), (0, fxl), (1, fxh))):
                                ins = pe.matmul(dst, wflat[:, bass.ds(e_in * EXP + (q * WE + k * F + c * P), P)],
                                                r[:, par, k, :],
                                                start=(k == 0 and i == 0), stop=(k == DK - 1 and i == 2))
                        if c % (FC // 2) == FC // 2 - 1:
                            ins.then_inc(f_h, 1)
                    if fhas(s, 4):
                        for i, (l, q) in enumerate(((hh, 2), (hh, 3), (hl, 2))):
                            ins = pe.matmul(ps[6 + par][:, 0:D], l[:, par, c, :],
                                            wflat[:, bass.ds(e_out * EXP + (q * WE + c * D), D)],
                                            start=(c == 0 and i == 0), stop=(c == FC - 1 and i == 2))
                        if c == FC - 1:
                            ins.then_inc(f_y, 1)
            fsteps(pe, fbody)

        @block.vector
        def _(dve):
            dve.memset(bd_all, 0.0).then_inc(bd_zero, 1)
            dve.wait_ge(bd_zero, 1)

            def evacuate(n):
                kind, arg, who = fills[n]
                if who != "D":
                    return
                bank = ps[n % 8]
                dve.wait_ge(filled, n + 1)
                if kind == "ctxT":
                    ins = dve.tensor_copy(ctxT[:, :, :].rearrange("p k m -> p (k m)"), bank[:, 0:DK * B * KEYS])
                elif kind in "kv":
                    bd = kbd if kind == "k" else vbd
                    a0, a1 = arg * PPB, min((arg + 1) * PPB, PAIRS)
                    for j in range(2):
                        rows = slice(j * HD, (j + 1) * HD)
                        ins = dve.tensor_copy(bd[rows, a0:a1, :, j, :],
                                              bank[rows, 0:(a1 - a0) * B * KEYS].rearrange(
                                                  "p (a b k) -> p a b k", b=B, k=KEYS))
                elif kind == "wqT":
                    ins = dve.tensor_copy(wqT[:, 2 * arg:2 * arg + 2, :].rearrange("p a d -> p (a d)"), bank[:, :])
                elif kind == "b1":
                    ins = dve.tensor_copy(b1c[:, :], bank[:, 0:NE * FC])
                elif kind == "a":
                    b, k, g = arg
                    h0, nh = BANKS[g]
                    cols = slice(h0 * KEYS, (h0 + nh) * KEYS)
                    dve.wait_ge(hi_done, his[n])
                    ins = dve.scalar_tensor_tensor(al[:, b, k, cols], bank[:, 0:nh * KEYS], SC_A / HD ** 0.5,
                                                   ah[:, b, k, cols], ALU.mult, ALU.subtract)
                elif kind == "x":
                    m = slice(2 * arg * P, (2 * arg + 2) * P)
                    dve.wait_ge(hi_done, his[n])
                    ins = dve.tensor_tensor(xtl[:, :, m], bank[:, :].rearrange("p (k m) -> p k m", k=DK),
                                            xth[:, :, m], ALU.subtract)
                elif kind == "vw":
                    b, i = arg
                    half = i // (PAIRS // 2)
                    if b:
                        dve.wait_ge(vw_st[half], 16 * b)
                    j = 2 * (i % (PAIRS // 2))
                    ins = dve.tensor_scalar(vwf[:, half, j:j + 2, :].rearrange("p h d -> p (h d)"),
                                            bank[0:KEYS, :], vsc[:, b:b + 1], None, ALU.mult)
                ins.then_inc(dve_out, 1)

            for n in range(of_kind["a"][0]):
                evacuate(n)
            for i in range(2):
                dve.wait_ge(ld_x[i], 32)
                for t in range(i * T // 2, (i + 1) * T // 2):
                    wait(dve, ln1_mv, t)
                    dve.bn_stats(bst[:, :], xall[:, t, :]).then_inc(ln1_st, 1)
                    dve.wait_ge(ln1_st, t + 1)
                    dve.bn_aggr(mv[:, t, :], bst[:, :]).then_inc(ln1_mv, 1)
                h = slice(i * T // 2, (i + 1) * T // 2)
                dve.wait_ge(ln1_mv, (i + 1) * T // 2)
                dve.tensor_scalar(rstd1[:, h], mv[:, h, 1], EPS, None, ALU.add).then_inc(ln1_ve, 1)
            dve.wait_ge(gate_ok, 1)
            dve.tensor_scalar(vsc[:, :], indT[:, :], gates[0:KEYS, 2:3], SC_VW, ALU.mult, ALU.mult)\
                .then_inc(vsc_ok, 1)
            dve.wait_ge(vsc_ok, 1)
            for n in of_kind["a"]:
                evacuate(n)
            for t in range(T):
                dve.wait_ge(ln1_rs, 1 + t // (T // 2))
                dve.tensor_scalar(xn[:, t, :], xall[:, t, :], mv[:, t, 0:1], rstd1[:, t:t + 1],
                                  ALU.subtract, ALU.mult).then_inc(ln1_xn, 1)
            for n in range(of_kind["x"][0], len(fills)):
                evacuate(n)
            pad = HK - (KC - 1) * P
            assert pad // 32 * 32 <= pad
            dve.wait_ge(ln1_xn, T)
            for r in range(2):
                dve.memset(probs[:, r, HK:HKP], 0.0).then_inc(ids_ok, 1)
            for b in range(B):
                dve.wait_ge(vw_ld[b], 32)
                dve.wait_ge(vw_hi, b + 1)
                dve.tensor_tensor(vwl[:, b, :, :], vwp[b], vwh[:, b, :, :], ALU.subtract).then_inc(vw_lo, 1)

            def body(s, quad):
                par = quad % 2
                t3, t4, other, r3 = s - 3, s - 4, 1 - par, (quad + 1) % ROWS

                def largest(g):
                    h0, nh = BANKS[g]
                    dve.wait_ge(s_sc, NB * s + g + 1)
                    dve.tensor_reduce(mx[:, h0:h0 + nh],
                                      S[g][:, 0:nh * KEYS].rearrange("p (h k) -> p h k", k=KEYS),
                                      X_AXIS, ALU.max).then_inc(s_mx, 1)

                def negated(g):
                    h0, nh = BANKS[g]
                    dve.wait_ge(s_mx, NB * s + g + 1)
                    dve.tensor_scalar(nb[:, h0:h0 + nh], mx[:, h0:h0 + nh], -1.0 / SC_A, None, ALU.mult)\
                        .then_inc(s_nb, 1)
                if has(s, 0):
                    largest(0)
                    negated(0)
                if has(s, 0):
                    for g in range(1, NB - 1):
                        largest(g)
                        negated(g)
                    largest(NB - 1)
                if has(s, 4):
                    dve.wait_ge(s_ro, t4 + 1)
                    dve.tensor_tensor(sc8[:, :], RS, br_b[:, :], ALU.add).then_inc(s_sb, 1)
                if has(s, 0):
                    negated(NB - 1)
                if has(s, 4):
                    wait_apart(dve, s_sb, t4 + 1)
                    dve.max(top8[:, :], sc8[:, :]).then_inc(s_tp, 1)
                if has(s, 3):
                    dve.wait_ge(s_pv, t3 + 1)
                    dve.wait_ge(ld_xr[other], (t3 - other) * 8 + 16)
                    wait(dve, row_free[r3], (t3 - r3) * (16 // ROWS))
                    dve.scalar_tensor_tensor(row[:, r3, 0:D], O[:, 0:D], 1.0 / (SC_P * SC_VW), xr[:, other, :],
                                             ALU.mult, ALU.add).then_inc(s_x2, 1)
                if has(s, 4):
                    wait_apart(dve, s_tp, t4 + 1)
                    dve.max_index(idx8[:, :], top8[:, :], sc8[:, :]).then_inc(s_ix, 1)
                if has(s, 3):
                    dve.tensor_scalar(row[:, r3, D + 2:D + 3], row[:, r3, D + 2:D + 3], float(ROWS // B * P), None,
                                      ALU.add).then_inc(ids_ok, 1)
                if has(s, 4):
                    dve.wait_ge(s_ix, t4 + 1)
                    dve.tensor_copy(idxf[:, :], idx8[:, 0:1]).then_inc(s_if, 1)
                if has(s, 3):
                    dve.wait_ge(s_x2, t3 + 1)
                    dve.bn_stats(bst[:, :], row[:, r3, 0:D]).then_inc(s_bs, 1)
                if has(s, 4):
                    dve.wait_ge(s_if, t4 + 1)
                    dve.tensor_scalar(onehot[:, :], iota8[:, :], idxf[:, 0:1], None, ALU.is_equal)\
                        .then_inc(s_oh, 1)
                if has(s, 3):
                    wait_apart(dve, s_bs, t3 + 1)
                    dve.bn_aggr(mv2[:, :], bst[:, :]).then_inc(s_ag, 1)
                if has(s, 3):
                    dve.wait_ge(s_ag, t3 + 1)
                    dve.tensor_scalar(ve2[:, :], mv2[:, 1:2], EPS, None, ALU.add).then_inc(s_ve, 1)
                if has(s, 3):
                    dve.wait_ge(s_rs, t3 + 1)
                    dve.scalar_tensor_tensor(row[:, r3, D + 1:D + 2], mv2[:, 0:1], -1.0, row[:, r3, D:D + 1],
                                             ALU.mult, ALU.mult).then_inc(s_nr, 1)
                    wait(dve, s_t2, t3)
                    dve.wait_ge(s_nr, t3 + 1)
                    dve.tensor_scalar(xn2[:, :], row[:, r3, 0:D], row[:, r3, D:D + 1], row[:, r3, D + 1:D + 2],
                                      ALU.mult, ALU.add).then_inc(s_xn, 1)
                if has_piece(s - 1):
                    p, pp = s - 1 - WLAG, par
                    dve.wait_ge(s_wh, p + 1)
                    a = (p - pp) * (EXP // 2) + pp * 2 * WE
                    dve.scalar_tensor_tensor(wflat[:, bass.ds(a + WE, WE)], stage[:, pp, :],
                                             (SC_W1, SC_W2)[pp], wflat[:, bass.ds(a, WE)],
                                             ALU.mult, ALU.subtract).then_inc(s_wl, 1)
                if has(s, 4):
                    dve.wait_ge(s_px, t4 + 1)
                    dve.tensor_tensor_reduce(junk8[:, :], onehot[:, :], RP, 1.0, 0.0, ALU.mult, ALU.add,
                                             rank[:, :]).then_inc(s_rk, 1)
                    dve.tensor_tensor(seen[:, :], seen[:, :], onehot[:, :], ALU.add).then_inc(s_ct, 1)
                    dve.wait_ge(s_rk, t4 + 1)
                    dve.scalar_tensor_tensor(pos[:, quad, :], idxf[:, :], float(CAP), rank[:, :],
                                             ALU.mult, ALU.add).then_inc(s_po, 1)
                if has(s, 0):
                    dve.wait_ge(s_ex, NB * (s + 1))
                    dve.reciprocal(rz[:, par, :], z[:, par, :]).then_inc(s_rz, 1)
                if has(s, 1):
                    t = s - 1
                    for g, (c0, n) in enumerate(PTB):
                        dve.wait_ge(s_ph, NB * t + g + 1)
                        dve.scalar_tensor_tensor(ptl[:, other, c0:c0 + n, :].rearrange("p c m -> p (c m)"),
                                                 PT[g][:, 0:n * P], SC_P,
                                                 pth[:, other, c0:c0 + n, :].rearrange("p c m -> p (c m)"),
                                                 ALU.mult, ALU.subtract).then_inc(s_pl, 1)
            steps(dve, body)

            tabn = [0]

            def link(ins):
                tabn[0] += 1
                ins.then_inc(tab, 1)
                dve.wait_ge(tab, tabn[0])
            dve.wait_ge(n_ok, 1)
            v = lambda t, a, b: t[:, 0:a * b].rearrange("p (a b) -> p a b", a=a)
            link(dve.tensor_tensor(v(tA, NE, T), RP.unsqueeze(2).to_broadcast([P, NE, T]), k128[:, :, :],
                                   ALU.is_gt))
            dve.tensor_tensor(ptab[:, :], RP, ecap[:, :], ALU.add)
            link(dve.tensor_reduce(nt_e[:, :], v(tA, NE, T), X_AXIS, ALU.add))
            link(dve.tensor_tensor(v(tA, NE, NE), nt_e[:, :].unsqueeze(1).to_broadcast([P, NE, NE]),
                                   incl[:, :, :], ALU.mult))
            link(dve.tensor_reduce(cum_e[:, :], v(tA, NE, NE), X_AXIS, ALU.add))
            link(dve.tensor_tensor(v(tA, NT, NE), cum_e[:, :].unsqueeze(1).to_broadcast([P, NT, NE]),
                                   jrow[:, :, :], ALU.is_le))
            dve.tensor_reduce(ej[:, :], v(tA, NT, NE), X_AXIS, ALU.add)
            link(dve.tensor_tensor(v(tB, NT, NE), v(tA, NT, NE),
                                   nt_e[:, :].unsqueeze(1).to_broadcast([P, NT, NE]), ALU.mult))
            link(dve.tensor_reduce(sj[:, :], v(tB, NT, NE), X_AXIS, ALU.add))
            dve.tensor_scalar(vj[:, :], ej[:, :], float(NE), float(P), ALU.is_lt, ALU.mult)
            dve.tensor_scalar(epad[:, 4:4 + NT], ej[:, :], float(NE - 1), None, ALU.min)
            link(dve.tensor_tensor(kj[:, :], jrow[:, :, 0], sj[:, :], ALU.subtract))
            link(dve.tensor_tensor(kj[:, :], kj[:, :], vj[:, :], ALU.mult))
            dve.tensor_scalar(etab[:, :], ej[:, :], float(NE - 1), None, ALU.min)
            digit = lambda d: epad[:, d:d + 2 * QP].rearrange("p (q two) -> p q two", two=2)[:, :, 0]
            link(dve.scalar_tensor_tensor(qacc[:, 0, :], digit(3), float(NE), digit(2), ALU.mult, ALU.add))
            link(dve.scalar_tensor_tensor(qacc[:, 1, :], qacc[:, 0, :], float(NE), digit(1), ALU.mult, ALU.add))
            link(dve.scalar_tensor_tensor(qtab[:, :], qacc[:, 1, :], float(NE), digit(0), ALU.mult, ALU.add))
            link(dve.scalar_tensor_tensor(rtab[:, :], ej[:, :], float(CAP), kj[:, :], ALU.mult, ALU.add))
            dve.memset(junk8[:, 0:1], 0.0).then_inc(tabs_ok, 1)

            def fbody(s, par):
                if fhas(s, 0):
                    wait(dve, f_xt, s - 1)
                    dve.wait_ge(ld_ra[par], (s - par) * 8 + 16)
                    dve.tensor_scalar(xnf[:, par, :], ra[:, par, 0:D], ra[:, par, D:D + 1], ra[:, par, D + 1:D + 2],
                                      ALU.mult, ALU.add).then_inc(f_xn, 1)
                if fhas(s, 5):
                    t, other = s - 5, 1 - par
                    e = dve.value_load(etab[0:1, bass.ds(t, 1)], min_val=0, max_val=NE - 1)
                    dve.wait_ge(f_y, t + 1)
                    if isinstance(s, int) and t == 0:
                        dve.wait_ge(ld_b2, 16)
                    wait(dve, f_yo, t)
                    dve.scalar_tensor_tensor(yt[:, :], ps[6 + other][:, 0:D], 1.0 / SC_W2,
                                             b2t[:, :, :].rearrange("p e d -> p (e d)")[:, bass.ds(e * D, D)],
                                             ALU.mult, ALU.add).then_inc(f_t1, 1)
                    dve.wait_ge(ld_rb[other], (t - other) * 8 + 16)
                    wait(dve, f_sc[other], (t - other) * 8)
                    dve.tensor_copy(ids[:, other, :], rb[:, other, D + 2:D + 3]).then_inc(f_id, 1)
                    dve.wait_ge(f_t1, t + 1)
                    dve.scalar_tensor_tensor(yo[:, other, :], yt[:, :], gates[:, 3:4], rb[:, other, 0:D],
                                             ALU.mult, ALU.add).then_inc(f_yo, 1)
                if fhas(s, 1):
                    t = s - 1
                    dve.wait_ge(f_xh, t + 1)
                    dve.tensor_tensor(fxl[:, 1 - par, :, :].rearrange("p k m -> p (k m)"), ps[1 - par][:, 0:D],
                                      fxh[:, 1 - par, :, :].rearrange("p k m -> p (k m)"),
                                      ALU.subtract).then_inc(f_xl, 1)
                if fhas(s, 2):
                    t = s - 2
                    dve.wait_ge(f_ge, 2 * (t + 1))
                    wait(dve, f_y, t - 1)
                    dve.tensor_copy(hh[:, par, :, :], hid[:, par, :, :]).then_inc(f_hh, 1)
            fsteps(dve, fbody)


_INS = ['x', 'ctx_1024', 'fside_BxS2_0', 'g_xattn', 'g_ffn', 'L0_xattn_Wq', 'L0_xattn_Wk', 'L0_xattn_Wv',
        'L0_xattn_Wo', 'L0_ffn_wr', 'L0_ffn_br', 'L0_ffn_w1', 'L0_ffn_b1', 'L0_ffn_w2', 'L0_ffn_b2']
_OUTS = [((2, 1024, 256), 'float32')]


def kernel(**inputs):
    import numpy as _np
    import concourse.bacc as _bacc
    from concourse import mybir as _mybir
    from concourse.bass_utils import run_bass_kernel_spmd as _run

    nc = _bacc.Bacc("TRN2", target_bir_lowering=False, num_devices=1)
    arrays, args = {}, []
    for name in _INS:
        a = _np.ascontiguousarray(inputs[name])
        arrays[f"in_{name}_dram"] = a
        args.append(nc.dram_tensor(f"in_{name}_dram", a.shape, _mybir.dt.from_np(a.dtype), kind="ExternalInput").ap())
    for i, (shape, dtype) in enumerate(_OUTS):
        dt = _mybir.dt.from_np(_np.dtype(dtype))
        args.append(nc.dram_tensor(f"out_{i}_dram", shape, dt, kind="ExternalOutput").ap())
    gated_cross_attention_then_routed_ffn(nc, *args)
    r = _run(nc, [arrays], core_ids=[0])
    got = tuple(r.results[0][f"out_{i}_dram"] for i in range(len(_OUTS)))
    return got[0]
```

```python
import concourse.bass as bass
from concourse import mybir
from contextlib import ExitStack

F32 = mybir.dt.float32
F16 = mybir.dt.float16
BF16 = mybir.dt.bfloat16
I32 = mybir.dt.int32
U32 = mybir.dt.uint32
ALU = mybir.AluOpType
ACT = mybir.ActivationFunctionType
X_AXIS = mybir.AxisListType.X

P = 128
EPS = 1e-5


def gated_cross_attention_then_routed_ffn(nc, x, ctx_in, ind, g_attn, g_ffn, wq, wk, wv, wo,
                                          wr, br, w1, b1, w2, b2, out):
    B, NQ, D = x.shape
    KEYS = ctx_in.shape[1]
    HD = 64
    H = wq.shape[1] // HD
    NE, _, F = w1.shape
    DK = D // P
    FC = F // P
    PAIRS = H // 2
    HK = H * KEYS
    KC = -(-HK // P)
    HKP = KC * P
    T = B * NQ // P
    assert B == 2 and D == 256 and T == 16 and F == 1024 and NE == 8
    HPB = 512 // KEYS
    BANKS = [(h0, min(HPB, H - h0)) for h0 in range(0, H, HPB)]
    NB = len(BANKS)
    PPB = HPB // 2
    SC_A = 64.0
    SC_P = 1024.0
    SC_VW = 16.0
    SC_W1 = 64.0
    SC_W2 = 256.0
    NTOK = B * NQ
    CAP = NTOK + P
    NT = (NTOK + NE * (P - 1)) // P
    ROWS = 4
    RW = D + 4
    PAD_ID = 4095.0
    rowbuf = nc.dram_tensor("rowbuf", (NE * CAP + P, RW), F32, kind="Internal").ap()
    PK = 2 * KEYS
    spans = [[(a, c * P - a * PK) for a in range(PAIRS) if -P < c * P - a * PK < PK] for c in range(KC)]
    OFF = -min(o for chunk in spans for _, o in chunk)
    WID = OFF + P + max(o for chunk in spans for _, o in chunk)
    outf = out.rearrange("b n d -> (b n) d")

    FLAG = 5
    ctx = ExitStack()
    with ctx:
        def sb(name, shape, dt):
            return ctx.enter_context(nc.sbuf_tensor(name, shape, dt))

        def sem(name):
            return ctx.enter_context(nc.semaphore(name))

        WE = 2 * F
        WALL = sb("WALL", [P, NE, 4, WE], F16)
        wflat = WALL[:, :, :, :].rearrange("p e q n -> p (e q n)")
        EXP = 4 * WE

        def early(expert, n, off=0):
            a = expert * EXP + 2 * off
            return wflat[:, a:a + 2 * n].bitcast(F32)
        NBD = PAIRS * B * 2 * KEYS
        bd_all = early(0, NBD)
        kbd = bd_all.rearrange("p (a b j k) -> p a b j k", a=PAIRS, b=B, j=2)
        wqT = early(0, PAIRS * D, NBD).rearrange("p (a d) -> p a d", a=PAIRS)
        vb1 = early(0, PAIRS * WID, NBD + PAIRS * D)
        assert 2 * (NBD + PAIRS * D + PAIRS * WID) <= 2 * EXP
        xn = early(2, T * D).rearrange("p (t d) -> p t d", t=T)
        xall = early(3, T * D).rearrange("p (t d) -> p t d", t=T)
        wk_s = early(4, DK * H * HD).rearrange("p (k n) -> p k n", k=DK)
        wv_s = early(4, DK * H * HD, DK * H * HD).rearrange("p (k n) -> p k n", k=DK)
        wq_s = early(5, DK * H * HD).rearrange("p (k n) -> p k n", k=DK)
        wo_s = early(5, PAIRS * D, PAIRS * D).rearrange("p (a d) -> p a d", a=PAIRS)
        A0 = 6 * EXP
        ah = wflat[:, A0:A0 + B * DK * HK].rearrange("p (b k n) -> p b k n", b=B, k=DK)
        al = wflat[:, A0 + B * DK * HK:A0 + 2 * B * DK * HK].rearrange("p (b k n) -> p b k n", b=B, k=DK)
        E0 = A0 + 2 * B * DK * HK
        probs = wflat[:, E0:E0 + 4 * HKP].bitcast(F32).rearrange("p (r n) -> p r n", r=2)
        assert E0 + 4 * HKP <= NE * EXP

        stage = sb("stage", [P, 2, WE], F32)
        stage_f = stage[:, :, :].rearrange("p r n -> p (r n)")
        vbs = [stage_f[:, 0:PAIRS * WID], vb1]
        vb = [v.rearrange("p (a n) -> p a n", a=PAIRS) for v in vbs]
        C0 = PAIRS * WID
        ctx_s = stage_f[0:KEYS, C0:C0 + B * D].rearrange("p (b d) -> p b d", b=B)
        ctxT = stage_f[:, C0 + B * D:C0 + B * D + DK * B * KEYS].rearrange("p (k m) -> p k m", k=DK)
        assert C0 + B * D + DK * B * KEYS <= 2 * WE
        row = sb("row", [P, ROWS, RW], F32)
        ident = sb("ident", [P, P], F32)
        upper = sb("upper", [P, P], BF16)
        ones = sb("ones", [P, P], BF16)
        wr_s = sb("wr_s", [P, DK, NE], F32)
        br_b = sb("br_b", [P, NE], F32)
        b1r = sb("b1r", [NE * FC, P], F32)
        b1c = sb("b1c", [P, NE * FC], F32)
        gates = sb("gates", [P, 4], F32)
        ind_b = sb("ind_b", [P, B * KEYS], F32)
        vsc = sb("vsc", [P, B, KEYS], F32)
        nmr1 = sb("nmr1", [P, T], F32)
        mv = sb("mv", [P, T, 2], F32)
        rstd1 = sb("rstd1", [P, T], F32)
        nhalf = sb("nhalf", [P, T], F32)
        bst1 = sb("bst1", [P, T, 6], F32)
        bst = sb("bst", [P, 6], F32)
        mv2 = sb("mv2", [P, 2], F32)
        ve2 = sb("ve2", [P, 1], F32)
        mx = sb("mx", [P, H], F32)
        nb = sb("nb", [P, H], F32)
        z = sb("z", [P, 2, H], F32)
        rz = sb("rz", [P, 2, H], F32)
        sc8 = sb("sc8", [P, NE], F32)
        top8 = sb("top8", [P, NE], F32)
        idx8 = sb("idx8", [P, NE], U32)
        idxf = sb("idxf", [P, 1], F32)
        iota8 = sb("iota8", [P, NE], F32)
        onehot = sb("onehot", [P, NE], BF16)
        seen = sb("seen", [P, NE], BF16)
        junk8 = sb("junk8", [P, NE], F32)
        rank = sb("rank", [P, 1], F32)
        pos = sb("pos", [P, ROWS, 1], I32)
        ids = sb("ids", [P, 2, 1], I32)
        k128 = sb("k128", [P, NE, T], F32)
        incl = sb("incl", [P, NE, NE], F32)
        jrow = sb("jrow", [P, NT, NE], F32)
        ecap = sb("ecap", [P, NE], F32)
        tA = sb("tA", [P, NT * NE], F32)
        tB = sb("tB", [P, NT * NE], F32)
        nt_e = sb("nt_e", [P, NE], F32)
        cum_e = sb("cum_e", [P, NE], F32)
        ej = sb("ej", [P, NT], F32)
        sj = sb("sj", [P, NT], F32)
        kj = sb("kj", [P, NT], F32)
        vj = sb("vj", [P, NT], F32)
        etab = sb("etab", [P, NT], I32)
        rtab = sb("rtab", [P, NT], I32)
        ptab = sb("ptab", [P, NE], I32)
        ppos = sb("ppos", [P, NE], I32)
        gelu_at = sb("gelu_at", [P, 1], F32)
        lane = sb("lane", [P, 1], F32)
        GROUP = 4
        DIGITS = GROUP + 2
        QP = -(-(NT + FLAG) // GROUP)
        assert NE ** DIGITS < 2 ** 24
        epad = sb("epad", [P, GROUP * QP + DIGITS], F32)
        qacc = sb("qacc", [P, 2, QP], F32)
        qtab = sb("qtab", [P, QP], I32)
        pad_rows = sb("pad_rows", [P, RW], F32)

        inner = ExitStack()

        def sbi(name, shape, dt):
            return inner.enter_context(nc.sbuf_tensor(name, shape, dt))
        xth = sbi("xth", [P, DK, T * P], F16)
        xtl = sbi("xtl", [P, DK, T * P], F16)
        vwh = sbi("vwh", [P, B, KC, D], F16)
        vwl = sbi("vwl", [P, B, KC, D], F16)
        pth = sbi("pth", [P, 2, KC, P], F16)
        ptl = sbi("ptl", [P, 2, KC, P], F16)
        xr = sbi("xr", [P, 2, D], F32)
        xn2 = sbi("xn2", [P, D], F32)
        xt2 = sbi("xt2", [P, DK, P], F32)
        inner.close()
        inner = ExitStack()
        b2t = sbi("b2t", [P, NE, D], F32)
        ra = sbi("ra", [P, 2, RW], F32)
        rb = sbi("rb", [P, 2, RW], F32)
        xnf = sbi("xnf", [P, 2, D], F32)
        fxh = sbi("fxh", [P, 2, DK, P], F16)
        fxl = sbi("fxl", [P, 2, DK, P], F16)
        hid = sbi("hid", [P, 2, FC, P], F32)
        hh = sbi("hh", [P, 2, FC, P], F16)
        hl = sbi("hl", [P, 2, FC, P], F16)
        yb = sbi("yb", [P, D], F32)
        yt = sbi("yt", [P, D], F32)
        yo = sbi("yo", [P, 2, D], F32)
        inner.close()

        ps = [ctx.enter_context(nc.psum_tensor(f"ps{i}", [P, 512], F32)) for i in range(8)]
        S = ps[0:NB]
        PT = ps[3:6]
        O = ps[6]
        R = ps[7]
        RT, RS, RP = R[:, 0:D], R[:, D:D + NE], O[:, D:D + NE]
        CPB = 4
        PTB = [(c0, min(CPB, KC - c0)) for c0 in range(0, KC, CPB)]

        ld_ctx, ld_wv, ld_wq, ld_wo = (sem(n) for n in ("ld_ctx", "ld_wv", "ld_wq", "ld_wo"))
        ld_wk = [sem("ld_wk0"), sem("ld_wk1")]
        ld_x = [sem("ld_x0"), sem("ld_x1")]
        ld_small = sem("ld_small")
        ld_b1 = sem("ld_b1")
        consts = sem("consts")
        passed = sem("passed")
        const_id = sem("const_id")
        bd_zero = sem("bd_zero")
        filled = sem("filled")
        act_out = sem("act_out")
        dve_out = sem("dve_out")
        gate_ok = sem("gate_ok")
        vsc_ok = sem("vsc_ok")
        ln1_st = sem("ln1_st")
        ln1_mv = sem("ln1_mv")
        ln1_ve = sem("ln1_ve")
        ln1_rs = sem("ln1_rs")
        ln1_xf = sem("ln1_xf")
        ln1_xn = sem("ln1_xn")
        vb_zero = sem("vb_zero")
        probs_pad = sem("probs_pad")
        vw_full = sem("vw_full")
        vw_hi = sem("vw_hi")
        vw_lo = sem("vw_lo")
        ln1_nr = sem("ln1_nr")
        s_sc = sem("s_sc")
        s_mx = sem("s_mx")
        s_nb = sem("s_nb")
        s_ex = sem("s_ex")
        ids_ok = sem("ids_ok")
        ids_set = sem("ids_set")
        s_rz = sem("s_rz")
        s_nm = sem("s_nm")
        s_pt = sem("s_pt")
        s_ph = sem("s_ph")
        s_pl = sem("s_pl")
        s_pv = sem("s_pv")
        s_x2 = sem("s_x2")
        s_bs = sem("s_bs")
        s_ag = sem("s_ag")
        s_ve = sem("s_ve")
        s_rs = sem("s_rs")
        s_nr = sem("s_nr")
        s_xn = sem("s_xn")
        s_t2 = sem("s_t2")
        s_tc = sem("s_tc")
        s_ro = sem("s_ro")
        s_sb = sem("s_sb")
        s_tp = sem("s_tp")
        s_ix = sem("s_ix")
        s_if = sem("s_if")
        s_oh = sem("s_oh")
        s_px = sem("s_px")
        s_rk = sem("s_rk")
        s_po = sem("s_po")
        s_ct = sem("s_ct")
        row_free = [sem(f"row_free{r}") for r in range(ROWS)]
        ld_xr = [sem("ld_xr0"), sem("ld_xr1")]
        w_in = [sem("w_in0"), sem("w_in1")]
        w_hi = sem("w_hi")
        w_lo = sem("w_lo")
        pad0 = sem("pad0")
        padded = sem("padded")
        pool_padded = sem("pool_padded")
        ld_b2 = sem("ld_b2")
        tab = sem("tab")
        tabs_ok = sem("tabs_ok")
        rows_ok = sem("rows_ok")
        pads_ok = sem("pads_ok")
        n_ok = sem("n_ok")
        ld_ra = [sem("ld_ra0"), sem("ld_ra1")]
        ld_rb = [sem("ld_rb0"), sem("ld_rb1")]
        f_xn = sem("f_xn")
        f_xt = sem("f_xt")
        f_xh = sem("f_xh")
        f_xl = sem("f_xl")
        f_h = sem("f_h")
        f_ge = sem("f_ge")
        f_hh = sem("f_hh")
        f_hl = sem("f_hl")
        f_y = sem("f_y")
        f_t1 = sem("f_t1")
        f_t2 = sem("f_t2")
        f_yo = sem("f_yo")
        f_id = sem("f_id")
        f_sc = [sem("f_sc0"), sem("f_sc1")]

        block = ctx.enter_context(nc.Block())

        NCONSTS = 14

        def wait(eng, s, v):
            if not isinstance(v, int) or v > 0:
                eng.wait_ge(s, v)

        def wait_apart(eng, s, v):
            wait(eng, s, v)
            eng.sem_inc(passed, 1)

        LAG = 4
        PEEL = 8
        def steps(eng, body):
            for s in range(PEEL):
                body(s, s % ROWS)
            with eng.Fori(PEEL // ROWS, T // ROWS) as q:
                for r in range(ROWS):
                    body(ROWS * q + r, r)
            for s in range(T, T + LAG):
                body(s, s % ROWS)

        VWF = KC // 2
        VW_STEPS = {0: range(0, 3), 1: range(3, VWF)}

        def vw_parts(s):
            return [(B - 1, i, i, ps[6 + i % 2]) for i in VW_STEPS.get(s, ())] if isinstance(s, int) else []

        def vw_at(i, b):
            return [v[:, b, 2 * i:2 * i + 2, :].rearrange("p c d -> p (c d)") for v in (vwh, vwl)]

        def has(s, lag):
            return not isinstance(s, int) or 0 <= s - lag < T

        FPEEL = 12

        def fsteps(eng, body):
            for s in range(FPEEL):
                body(s, s % GROUP)
            with eng.Fori(FPEEL // GROUP, NT // GROUP) as q:
                for r in range(GROUP):
                    body(GROUP * q + r, r)
            for s in range(NT - NT % GROUP, NT + FLAG):
                body(s, s % GROUP)

        PAD_SPLIT = (3, 5)
        FIRST = 4

        def fhas(s, lag):
            return not isinstance(s, int) or 0 <= s - lag < NT

        NP = 2 * NE
        HIGH_AT = {1: 0, 2: 1, 3: 2, 5: 3, 16: 4, 17: 5}
        LOW_AT = {2: (0, 0, 1), 3: (1, 0, 1), 4: (2, 0, 2), 5: (2, 1, 2), 6: (3, 0, 2), 7: (3, 1, 2), 17: (4, 0, 1)}
        EARLY = 7
        LOWS = 1 + max(p for p, _, _ in LOW_AT.values())
        AT_FSTEP = {p - EARLY + 1: p for p in range(EARLY, NP)}
        assert max(AT_FSTEP) < FPEEL - 1
        assert all(s + 1 <= p // 2 + (2, 4)[p % 2] for s, p in AT_FSTEP.items())

        def load_piece(p):
            if p >= 2:
                nc.sync.wait_ge(w_hi, p - 1)
                nc.sync.wait_ge(w_lo, p - 1)
            if p % 2 == 0:
                src, dst = w1[p // 2].rearrange("(k p) n -> p k n", p=P), stage[:, 0, :].rearrange(
                    "p (k n) -> p k n", k=DK)
            else:
                src, dst = w2[p // 2].rearrange("(c p) d -> p c d", p=P), stage[:, 1, :].rearrange(
                    "p (c d) -> p c d", c=FC)
            nc.sync.dma_start(dst, src).then_inc(w_in[p % 2], 16)

        def halves(p):
            place = WALL[:, p // 2, 2 * (p % 2):2 * (p % 2) + 2, :].rearrange("p q n -> p (q n)")
            if p % 2 == 0:
                return place[:, 0:WE], place[:, WE:2 * WE], stage[:, 0, :]
            place = place.rearrange("p (c q d) -> p c q d", q=2, d=D)
            return place[:, :, 0, :], place[:, :, 1, :], stage[:, 1, :].rearrange("p (c d) -> p c d", d=D)

        def high_of_piece(p):
            nc.scalar.wait_ge(w_in[p % 2], 16 * (p // 2 + 1))
            hi, _, src = halves(p)
            nc.scalar.activation(hi, src, ACT.Copy, scale=(SC_W1, SC_W2)[p % 2]).then_inc(w_hi, 1)

        def low_of_piece(p, part=0, parts=1):
            nc.vector.wait_ge(w_hi, p + 1)
            hi, lo, src = halves(p)
            n = src.shape[1] // parts
            hi, lo, src = (v[:, part * n:(part + 1) * n] for v in (hi, lo, src))
            ins = nc.vector.scalar_tensor_tensor(lo, src, (SC_W1, SC_W2)[p % 2], hi, ALU.mult, ALU.subtract)
            if part == parts - 1:
                ins.then_inc(w_lo, 1)

        fills = [("ctxT", 0, "D")]
        fills += [("k", g, "D") for g in range(NB)]
        fills += [("wqT", g, "A") for g in range(4)]
        fills += [("b1", 0, "A")]
        fills += [("a", (b, k, g), "D") for b in range(B) for k in range(DK) for g in range(NB)]
        fills += [("v", g, "D") for g in range(NB)]
        fills += [("x", g, "D") for g in range(T // 2)]
        fills += [("vw", (b, i), "D") for b in range(B - 1) for i in range(KC // 2)]
        released = []
        n_rel = {"A": 0, "D": 0}
        for kind, _, who in fills:
            n_rel[who] += 1
            released.append((who, n_rel[who]))
        hi_done = sem("hi_done")
        his = {}
        for n, (kind, _, _) in enumerate(fills):
            if kind in ("a", "x", "vw"):
                his[n] = len(his) + 1
        of_kind = {}
        for n, (kind, arg, _) in enumerate(fills):
            of_kind.setdefault(kind, []).append(n)

        LN1_AT = of_kind["a"][11]

        def emptied(eng, n):
            who, v = released[n]
            eng.wait_ge(act_out if who == "A" else dve_out, v)

        def all_emptied(eng, kind):
            for who in "AD":
                v = max([released[n][1] for n in of_kind[kind] if released[n][0] == who], default=0)
                if v:
                    eng.wait_ge(act_out if who == "A" else dve_out, v)

        @block.sync
        def _(sp):
            sp.dma_start(ctx_s[:, :, :], ctx_in.rearrange("b k d -> k b d")).then_inc(ld_ctx, 16)
            for i, g in enumerate((slice(0, PPB * P), slice(PPB * P, H * HD))):
                sp.dma_start(wk_s[:, :, g], wk.rearrange("(k p) n -> p k n", p=P)[:, :, g]).then_inc(ld_wk[i], 16)
            xv = x.rearrange("b (n p) d -> p n b d", p=P)
            xa = xall.rearrange("p (n b) d -> p n b d", b=B)
            sp.dma_start(wq_s, wq.rearrange("(k p) n -> p k n", p=P)).then_inc(ld_wq, 16)
            for i in range(2):
                for b in range(B):
                    sp.dma_start(xa[:, i * T // 4:(i + 1) * T // 4, b, :],
                                 xv[:, i * T // 4:(i + 1) * T // 4, b, :]).then_inc(ld_x[i], 16)
            sp.dma_start(wv_s, wv.rearrange("(k p) n -> p k n", p=P)).then_inc(ld_wv, 16)
            sp.dma_start(wo_s, wo.rearrange("(a p) d -> p a d", p=P)).then_inc(ld_wo, 16)
            sp.wait_ge(filled, len(fills))
            for p in range(EARLY):
                load_piece(p)
            sp.wait_ge(s_pv, T)
            sp.dma_start(b2t[:, :, :].rearrange("p e d -> p (e d)"),
                         b2.rearrange("e d -> (e d)").unsqueeze(0).to_broadcast([P, NE * D])).then_inc(ld_b2, 16)
            sp.wait_ge(pad0, 1)
            sp.dma_start(rowbuf[NE * CAP:NE * CAP + P, :], pad_rows[:, :]).then_inc(padded, 16)
            sp.wait_ge(pads_ok, 1)
            with sp.Fori(0, PAD_SPLIT[0]) as e:
                r = sp.value_load(ptab[0:1, bass.ds(e, 1)], min_val=0, max_val=NE * CAP)
                sp.dma_start(rowbuf[bass.ds(r, P), :], pad_rows[:, :]).then_inc(padded, 16)
            sp.wait_ge(rows_ok, 1)

            def load_rows(t, buf, sems):
                r = sp.value_load(rtab[0:1, bass.ds(t, 1)], min_val=0, max_val=NE * CAP)
                if isinstance(t, int) and t == 0:
                    sp.wait_ge(padded, 16 * (PAD_SPLIT[1] + 1))
                    sp.wait_ge(pool_padded, 16 * (NE - PAD_SPLIT[1]))
                    for i in range(ROWS):
                        sp.wait_ge(row_free[i], 16 * (T // ROWS))
                sp.dma_start(buf, rowbuf[bass.ds(r, P), :]).then_inc(sems, 16)
            for t in range(FIRST):
                wait(sp, f_xn, t - 1)
                load_rows(t, ra[:, t % 2, :], ld_ra[t % 2])
                if t in (1, 2):
                    load_piece(EARLY + t - 1)

            def fbody(s, quad):
                par = quad % 2
                if not isinstance(s, int) or FIRST <= s + 1 < NT:
                    wait(sp, f_xn, s)
                    load_rows(s + 1, ra[:, 1 - par, :], ld_ra[1 - par])
                if fhas(s, 4):
                    t = s - 4
                    wait(sp, f_yo, t - 1)
                    wait(sp, f_id, t - 1)
                    load_rows(t, rb[:, par, :], ld_rb[par])
                if isinstance(s, int) and s - 1 in AT_FSTEP and AT_FSTEP[s - 1] + 2 < NP:
                    load_piece(AT_FSTEP[s - 1] + 2)
            fsteps(sp, fbody)

        @block.gpsimd
        def _(pool):
            pool.memset(ident[:, :], 0.0).then_inc(const_id, 1)
            pool.memset(upper[:, :], 1.0).then_inc(const_id, 1)
            pool.memset(incl[:, :, :], 1.0).then_inc(const_id, 1)
            pool.wait_ge(const_id, 3)
            pool.affine_select(out=ident[:, :], in_=ident[:, :], compare_op=ALU.not_equal, fill=1.0,
                               base=0, pattern=[[-1, P]], channel_multiplier=1).then_inc(consts, 1)
            pool.affine_select(out=upper[:, :], in_=upper[:, :], compare_op=ALU.is_gt, fill=0.0,
                               base=0, pattern=[[1, P]], channel_multiplier=-1).then_inc(consts, 1)
            pool.affine_select(out=incl[:, :, :], in_=incl[:, :, :], compare_op=ALU.is_ge, fill=0.0,
                               base=0, pattern=[[1, NE], [-1, NE]], channel_multiplier=0).then_inc(consts, 1)
            pool.memset(ones[:, :], 1.0).then_inc(consts, 1)
            pool.memset(seen[:, :], 0.0).then_inc(consts, 1)
            pool.memset(nhalf[:, :], -0.5).then_inc(consts, 1)
            pool.memset(epad[:, :], 0.0).then_inc(consts, 1)
            iota = lambda dst, pattern, base, cm: pool.iota(
                dst, pattern, base=base, channel_multiplier=cm,
                allow_small_or_imprecise_dtypes=True).then_inc(consts, 1)
            iota(iota8[:, :], [[1, NE]], 0, 0)
            iota(k128[:, :, :], [[0, NE], [P, T]], 0, 0)
            pool.wait_ge(consts, 9)
            pool.memset(k128[:, :, 0:1], -1.0).then_inc(consts, 1)
            iota(jrow[:, :, :], [[1, NT], [0, NE]], 0, 0)
            iota(ecap[:, :], [[CAP, NE]], 0, 0)
            iota(lane[:, :], [[0, 1]], 0, 1)
            for r in range(ROWS):
                pool.iota(row[:, r, D + 2:D + 3], [[0, 1]], base=(r % B) * NQ + (r // B - ROWS // B) * P,
                          channel_multiplier=1, allow_small_or_imprecise_dtypes=True).then_inc(ids_set, 1)
            pool.wait_ge(ids_set, ROWS)
            pool.memset(row[:, :, D + 3:D + 4], 0.0).then_inc(consts, 1)
            pool.memset(pad_rows[:, :], 0.0).then_inc(const_id, 1)
            pool.wait_ge(const_id, 4)
            pool.memset(pad_rows[:, D + 2:D + 3], PAD_ID).then_inc(pad0, 1)
            for v in vbs:
                pool.memset(v, 0.0).then_inc(vb_zero, 1)
            def power(n):
                h = slice((n - 1) * T // 2, n * T // 2)
                pool.wait_ge(ln1_ve, n)
                pool.tensor_tensor(rstd1[:, h], rstd1[:, h], nhalf[:, h], ALU.pow).then_inc(ln1_rs, 1)
            power(1)
            pool.wait_ge(ln1_nr, 1)
            for t in range(T // 2):
                if t == T // 4:
                    power(2)
                pool.tensor_scalar(xn[:, t, :], xall[:, t, :], rstd1[:, t:t + 1], nmr1[:, t:t + 1],
                                   ALU.mult, ALU.add).then_inc(ln1_xf, 1)

            def body(s, quad):
                par = quad % 2
                if has(s, 3):
                    pool.wait_ge(s_ve, s - 3 + 1)
                    pool.tensor_tensor(row[:, (quad + 1) % ROWS, D:D + 1], ve2[:, :], nhalf[:, 0:1], ALU.pow)\
                        .then_inc(s_rs, 1)
                if has(s, 0):
                    pool.wait_ge(s_rz, s + 1)
                    pv = probs[:, par, 0:HK].rearrange("p (h k) -> p h k", h=H)
                    pool.tensor_tensor(pv, pv, rz[:, par, :].unsqueeze(2).to_broadcast([P, H, KEYS]),
                                       ALU.mult).then_inc(s_nm, 1)
                if has(s, 4):
                    wait_apart(pool, s_po, s - 4 + 1)
                    pool.indirect_dma_start(rowbuf[:, :], bass.IndirectOffsetOnAxis(pos[:, quad, :], 0),
                                            row[:, quad, :], None).then_inc(row_free[quad], 16)
            steps(pool, body)
            pool.wait_ge(pads_ok, 2)
            for e in range(PAD_SPLIT[1], NE):
                pool.indirect_dma_start(rowbuf[:, :], bass.IndirectOffsetOnAxis(ppos[:, e:e + 1], 0),
                                        pad_rows[:, :], None).then_inc(pool_padded, 16)

            def fbody(s, quad):
                par = quad % 2
                if fhas(s, 2):
                    t = s - 2
                    pool.wait_ge(f_hh, t + 1)
                    wait(pool, f_y, t - 1)
                    pool.tensor_tensor(hl[:, par, :, :], hid[:, par, :, :], hh[:, par, :, :],
                                       ALU.subtract).then_inc(f_hl, 1)
                if fhas(s, 5):
                    pool.wait_ge(f_id, s - 5 + 1)
                    pool.wait_ge(f_yo, s - 5 + 1)
                    pool.sem_inc(passed, 1)
                    pool.indirect_dma_start(outf[:, :], bass.IndirectOffsetOnAxis(ids[:, 1 - par, :], 0),
                                            yo[:, 1 - par, :], None, bounds_check=NTOK - 1,
                                            oob_is_err=False).then_inc(f_sc[1 - par], 16)
            fsteps(pool, fbody)
            for i in range(2):
                pool.wait_ge(f_sc[i], 16 * ((NT + 1 - i) // 2))

        @block.scalar
        def _(act):
            act.dma_start(gates[:, 0:1], g_attn.unsqueeze(0).to_broadcast([P, 1])).then_inc(ld_small, 16)
            act.dma_start(gates[:, 1:2], g_ffn.unsqueeze(0).to_broadcast([P, 1])).then_inc(ld_small, 16)
            act.dma_start(ind_b[:, :], ind.rearrange("b k -> (b k)").unsqueeze(0).to_broadcast([P, B * KEYS]))\
                .then_inc(ld_small, 16)
            act.dma_start(wr_s[:, :, :], wr.rearrange("(k p) e -> p k e", p=P)).then_inc(ld_small, 16)
            act.dma_start(br_b[:, :], br.unsqueeze(0).to_broadcast([P, NE])).then_inc(ld_small, 16)
            act.dma_start(b1r[:, :], b1.rearrange("e (c p) -> (e c) p", p=P)).then_inc(ld_b1, 16)
            act.wait_ge(ld_small, 80)
            act.activation(gates[:, 2:4], gates[:, 0:2], ACT.Tanh).then_inc(gate_ok, 1)
            for n, (kind, arg, who) in enumerate(fills):
                bank = ps[n % 8]
                if kind == "wqT":
                    act.wait_ge(filled, n + 1)
                    act.activation(wqT[:, 2 * arg:2 * arg + 2, :].rearrange("p a d -> p (a d)"),
                                   bank[:, :], ACT.Copy).then_inc(act_out, 1)
                elif kind == "b1":
                    act.wait_ge(filled, n + 1)
                    act.activation(b1c[:, :], bank[:, 0:NE * FC], ACT.Copy).then_inc(act_out, 1)
                elif kind == "a":
                    b, k, g = arg
                    h0, nh = BANKS[g]
                    act.wait_ge(filled, n + 1)
                    act.activation(ah[:, b, k, h0 * KEYS:(h0 + nh) * KEYS], bank[:, 0:nh * KEYS],
                                   ACT.Copy, scale=SC_A / HD ** 0.5).then_inc(hi_done, 1)
                elif kind == "x":
                    act.wait_ge(filled, n + 1)
                    act.activation(xth[:, :, 2 * arg * P:(2 * arg + 2) * P],
                                   bank[:, :].rearrange("p (k m) -> p k m", k=DK), ACT.Copy).then_inc(hi_done, 1)
                elif kind == "vw":
                    b, i = arg
                    act.wait_ge(filled, n + 1)
                    act.activation(vwh[:, b, 2 * i:2 * i + 2, :].rearrange("p c d -> p (c d)"), bank[:, :],
                                   ACT.Copy).then_inc(hi_done, 1)
                if n == LN1_AT:
                    act.wait_ge(ln1_nr, 2)
                    for t in range(T // 2, T):
                        act.activation(xn[:, t, :], xall[:, t, :], ACT.Identity, bias=nmr1[:, t:t + 1],
                                       scale=rstd1[:, t:t + 1]).then_inc(ln1_xn, 1)

            def body(s, quad):
                par = quad % 2
                if has(s, 0):
                    wait(act, s_pt, NB * (s - 1))
                    wait(act, s_rz, s - 1)
                    for g, (h0, nh) in enumerate(BANKS):
                        act.wait_ge(s_nb, NB * s + g + 1)
                        for h in range(h0, h0 + nh):
                            ins = act.activation(probs[:, par, h * KEYS:(h + 1) * KEYS],
                                                 S[g][:, (h - h0) * KEYS:(h - h0 + 1) * KEYS], ACT.Exp,
                                                 bias=nb[:, h:h + 1], scale=1.0 / SC_A,
                                                 accum_out=z[:, par, h:h + 1])
                        ins.then_inc(s_ex, 1)
                        for b, i, n, bank in vw_parts(s)[g:(g + 1 if g < NB - 1 else VWF)]:
                            act.wait_ge(vw_full, n + 1)
                            act.activation(vw_at(i, b)[0], bank[:, :], ACT.Copy).then_inc(vw_hi, 1)
                if has(s, 2):
                    t = s - 2
                    wait(act, s_x2, t - 1)
                    bt = par
                    if isinstance(s, int):
                        src = x[bt, (t // 2) * P:(t // 2 + 1) * P, :]
                    else:
                        src = x[bt, bass.ds((t - bt) * (P // 2), P), :]
                    act.dma_start(xr[:, par, :], src).then_inc(ld_xr[par], 16)
                if has(s, 1):
                    t = s - 1
                    wait(act, s_pv, t - 1)
                    for g, (c0, n) in enumerate(PTB):
                        act.wait_ge(s_pt, NB * t + g + 1)
                        act.activation(pth[:, 1 - par, c0:c0 + n, :].rearrange("p c m -> p (c m)"),
                                       PT[g][:, 0:n * P], ACT.Copy, scale=SC_P).then_inc(s_ph, 1)
                if isinstance(s, int) and s in HIGH_AT and s < T:
                    high_of_piece(HIGH_AT[s])
                if has(s, 3):
                    act.wait_ge(s_t2, s - 3 + 1)
                    wait(act, s_ro, s - 3)
                    act.activation(xt2[:, :, :].rearrange("p k m -> p (k m)"), RT, ACT.Copy).then_inc(s_tc, 1)
                if isinstance(s, int) and s in HIGH_AT and s >= T:
                    high_of_piece(HIGH_AT[s])
            steps(act, body)
            act.wait_ge(pad0, 1)
            act.wait_ge(pads_ok, 1)
            with act.Fori(*PAD_SPLIT) as e:
                r = act.value_load(ptab[0:1, bass.ds(e, 1)], min_val=0, max_val=NE * CAP)
                act.dma_start(rowbuf[bass.ds(r, P), :], pad_rows[:, :]).then_inc(padded, 16)
            act.wait_ge(s_sc, NB * T)
            act.wait_ge(s_pt, NB * T)
            for p in range(len(HIGH_AT), EARLY):
                high_of_piece(p)
            act.activation(gelu_at[:, :], nhalf[:, 0:1], ACT.Gelu)
            act.wait_ge(tabs_ok, 1)

            def fbody(s, quad):
                par = quad % 2
                if fhas(s, 1):
                    t = s - 1
                    act.wait_ge(f_xt, t + 1)
                    wait(act, f_h, 2 * (t - 1))
                    act.activation(fxh[:, 1 - par, :, :].rearrange("p k m -> p (k m)"), ps[1 - par][:, 0:D],
                                   ACT.Copy).then_inc(f_xh, 1)
                if fhas(s, 2):
                    t = s - 2
                    e = act.value_load(etab[0:1, bass.ds(t, 1)], min_val=0, max_val=NE - 1)
                    wait(act, f_hl, t - 1)
                    for g in range(2):
                        act.wait_ge(f_h, 2 * t + g + 1)
                        for c in range(FC // 2):
                            cc = g * FC // 2 + c
                            ins = act.activation(hid[:, par, cc, :], ps[2 + 2 * par + g][:, c * P:(c + 1) * P],
                                                 ACT.Gelu, bias=b1c[:, bass.ds(e * FC + cc, 1)],
                                                 scale=1.0 / SC_W1)
                        ins.then_inc(f_ge, 1)
                if isinstance(s, int) and s in AT_FSTEP:
                    high_of_piece(AT_FSTEP[s])
            fsteps(act, fbody)

        @block.tensor
        def _(pe):
            pe.wait_ge(consts, NCONSTS)
            for n, (kind, arg, who) in enumerate(fills):
                bank = ps[n % 8]
                if n >= 8:
                    emptied(pe, n - 8)
                if kind == "ctxT":
                    pe.wait_ge(ld_ctx, 16)
                    for k in range(DK):
                        for b in range(B):
                            c = (k * B + b) * KEYS
                            ins = pe.transpose(bank[:, c:c + KEYS], ctx_s[:, b, k * P:(k + 1) * P],
                                               ident[0:KEYS, 0:KEYS])
                elif kind in "kv":
                    if arg == 0:
                        emptied(pe, of_kind["ctxT"][0])
                        pe.wait_ge(ld_wk[0] if kind == "k" else ld_wv, 16)
                    elif kind == "k":
                        pe.wait_ge(ld_wk[1], 16)
                    w = wk_s if kind == "k" else wv_s
                    pairs = range(arg * PPB, min((arg + 1) * PPB, PAIRS))
                    for i, a in enumerate(pairs):
                        for k in range(DK):
                            ins = pe.matmul(bank[:, i * B * KEYS:(i + 1) * B * KEYS],
                                            w[:, k, a * P:(a + 1) * P], ctxT[:, k, :],
                                            start=(k == 0), stop=(k == DK - 1))
                elif kind == "wqT":
                    if arg == 0:
                        pe.wait_ge(ld_wq, 16)
                    for i in range(2):
                        for k in range(DK):
                            a = 2 * arg + i
                            ins = pe.transpose(bank[:, (i * DK + k) * P:(i * DK + k + 1) * P],
                                               wq_s[:, k, a * P:(a + 1) * P], ident[:, :])
                elif kind == "b1":
                    pe.wait_ge(ld_b1, 16)
                    ins = pe.transpose(bank[:, 0:NE * FC], b1r[:, :], ident[0:NE * FC, 0:NE * FC])
                elif kind == "a":
                    b, k, g = arg
                    if n == of_kind["a"][0]:
                        all_emptied(pe, "wqT")
                        all_emptied(pe, "k")
                    for i, a in enumerate(range(g * PPB, min((g + 1) * PPB, PAIRS))):
                        ins = pe.matmul(bank[:, i * 2 * KEYS:(i + 1) * 2 * KEYS], wqT[:, a, k * P:(k + 1) * P],
                                        kbd[:, a, b, :, :].rearrange("p j k -> p (j k)"), start=True, stop=True)
                elif kind == "x":
                    first = 2 * arg < T // 2
                    pe.wait_ge(ln1_xf if first else ln1_xn, 2 * arg + 2 - (0 if first else T // 2))
                    for k in range(DK):
                        for i in range(2):
                            ins = pe.transpose(bank[:, (k * 2 + i) * P:(k * 2 + i + 1) * P],
                                               xn[:, 2 * arg + i, k * P:(k + 1) * P], ident[:, :])
                elif kind == "vw":
                    b, a = arg
                    if n == of_kind["vw"][0]:
                        all_emptied(pe, "v")
                        pe.wait_ge(ld_wo, 16)
                    for j in range(2):
                        chunk = spans[2 * a + j]
                        for i, (pair, o) in enumerate(chunk):
                            ins = pe.matmul(bank[:, j * D:(j + 1) * D], vb[b][:, pair, OFF + o:OFF + o + P],
                                            wo_s[:, pair, :], start=(i == 0), stop=(i == len(chunk) - 1))
                ins.then_inc(filled, 1)
            last_fill = {n % 8: n for n in range(len(fills))}
            for bank in range(NB):
                emptied(pe, last_fill[bank])

            def router(s):
                if has(s, 4):
                    t = s - 4
                    pe.wait_ge(s_tc, t + 1)
                    for k in range(DK):
                        ins = pe.matmul(RS, xt2[:, k, :], wr_s[:, k, :], start=(k == 0), stop=(k == DK - 1))
                    ins.then_inc(s_ro, 1)

            def body(s, quad):
                par = quad % 2
                if not has(s, 0):
                    router(s)
                if has(s, 0):
                    xs = bass.ds(s * P, P)
                    for g, (h0, nh) in enumerate(BANKS):
                        if g == NB - 1:
                            router(s)
                        cols = slice(h0 * KEYS, (h0 + nh) * KEYS)
                        wait(pe, s_ex, NB * (s - 1) + g + 1)
                        for k in range(DK):
                            for i, (l, r) in enumerate(((xth, ah), (xth, al), (xtl, ah))):
                                ins = pe.matmul(S[g][:, 0:nh * KEYS], l[:, k, xs], r[:, par, k, cols],
                                                start=(k == 0 and i == 0), stop=(k == DK - 1 and i == 2))
                        ins.then_inc(s_sc, 1)
                if isinstance(s, int) and s == 0:
                    for bank in range(NB, 8):
                        emptied(pe, last_fill[bank])
                if has(s, 1):
                    t = s - 1
                    pe.wait_ge(s_nm, t + 1)
                    for g, (c0, n) in enumerate(PTB):
                        wait(pe, s_pl, NB * (t - 1) + g + 1)
                        for i in range(n):
                            c = c0 + i
                            ins = pe.transpose(PT[g][:, i * P:(i + 1) * P], probs[:, 1 - par, c * P:(c + 1) * P],
                                               ident[:, :])
                        ins.then_inc(s_pt, 1)
                for b, i, n, bank in vw_parts(s):
                    wait(pe, vw_lo, n - 1)
                    for j in range(2):
                        chunk = spans[2 * i + j]
                        for m, (pair, o) in enumerate(chunk):
                            ins = pe.matmul(bank[:, j * D:(j + 1) * D], vb[b][:, pair, OFF + o:OFF + o + P],
                                            wo_s[:, pair, :], start=(m == 0), stop=(m == len(chunk) - 1))
                    ins.then_inc(vw_full, 1)
                if has(s, 2):
                    t = s - 2
                    if isinstance(s, int) and s <= B + 1:
                        pe.wait_ge(vw_lo, VWF)
                    wait(pe, s_x2, t)
                    pb = par
                    for g, (c0, n) in enumerate(PTB):
                        pe.wait_ge(s_pl, NB * t + g + 1)
                        for c in range(c0, c0 + n):
                            for i, (l, r) in enumerate(((pth, vwh), (pth, vwl), (ptl, vwh))):
                                ins = pe.matmul(O[:, 0:D], l[:, pb, c, :], r[:, pb, c, :],
                                                start=(c == 0 and i == 0), stop=(c == KC - 1 and i == 2))
                    ins.then_inc(s_pv, 1)
                if has(s, 4):
                    t = s - 4
                    pe.wait_ge(s_oh, t + 1)
                    pe.matmul(RP, upper[:, :], onehot[:, :], start=True, stop=False)
                    pe.matmul(RP, ones[:, :], seen[:, :], start=False, stop=True).then_inc(s_px, 1)
                if has(s, 3):
                    t = s - 3
                    pe.wait_ge(s_xn, t + 1)
                    for k in range(DK):
                        ins = pe.transpose(R[:, k * P:(k + 1) * P], xn2[:, k * P:(k + 1) * P], ident[:, :])
                    ins.then_inc(s_t2, 1)
            steps(pe, body)
            pe.wait_ge(s_ct, T)
            pe.matmul(RP, ones[:, :], seen[:, :], start=True, stop=True).then_inc(n_ok, 1)
            pe.wait_ge(tabs_ok, 1)
            packed = [None]

            def part_of(e, at, n):
                return wflat[:, at:at + (NE - 1) * EXP + n][:, bass.ds(e * EXP, n)]

            def fbody(s, quad):
                par = quad % 2
                if quad == 0:
                    group = s // GROUP
                    packed[0] = pe.value_load(qtab[0:1, bass.ds(group, 1)], min_val=0,
                                              max_val=NE ** DIGITS - 1)

                def e_of(digit):
                    return packed[0] // NE ** digit % NE
                if fhas(s, 1):
                    t = s - 1
                    pe.wait_ge(f_xn, t + 1)
                    wait(pe, f_xl, t - 1)
                    for k in range(DK):
                        ins = pe.transpose(ps[1 - par][:, k * P:(k + 1) * P], xnf[:, 1 - par, k * P:(k + 1) * P],
                                           ident[:, :])
                    ins.then_inc(f_xt, 1)
                if fhas(s, 4):
                    t = s - 4
                    e_out = e_of(quad)
                    if isinstance(s, int) and s < FPEEL:
                        pe.wait_ge(w_lo, 2 * e_out + 2)
                    pe.wait_ge(f_hl, t + 1)
                    wait(pe, f_yo, t - 1)
                if fhas(s, 2):
                    t = s - 2
                    e_in = e_of(2 + quad)
                    if isinstance(s, int) and s < FPEEL:
                        pe.wait_ge(w_lo, 2 * e_in + 1)
                    pe.wait_ge(f_xl, t + 1)
                    wait(pe, f_ge, 2 * (t - 1))
                for c in range(FC):
                    if fhas(s, 2):
                        hb = ps[2 + 2 * par + c // (FC // 2)]
                        dst = hb[:, (c % (FC // 2)) * P:(c % (FC // 2) + 1) * P]
                        for k in range(DK):
                            for i, (q, r) in enumerate(((0, fxh), (0, fxl), (1, fxh))):
                                ins = pe.matmul(dst, part_of(e_in, q * WE + k * F + c * P, P),
                                                r[:, par, k, :],
                                                start=(k == 0 and i == 0), stop=(k == DK - 1 and i == 2))
                        if c % (FC // 2) == FC // 2 - 1:
                            ins.then_inc(f_h, 1)
                    if fhas(s, 4):
                        at = 2 * WE + c * 2 * D
                        wide = (ps[6 + par][:, :], hh[:, par, c, :], 2 * D)
                        narrow = (ps[6 + par][:, 0:D], hl[:, par, c, :], D)
                        for i, (dst, l, n) in enumerate((wide, narrow) if c < FC - 1 else (narrow, wide)):
                            ins = pe.matmul(dst, l, part_of(e_out, at, n), start=(c == 0 and i == 0),
                                            stop=(c == FC - 1 and i == 1))
                        if c == FC - 1:
                            ins.then_inc(f_y, 1)
                if isinstance(s, int) and s == FPEEL - 1:
                    pe.wait_ge(w_lo, NP)
            fsteps(pe, fbody)

        @block.vector
        def _(dve):
            dve.memset(bd_all, 0.0).then_inc(bd_zero, 1)
            dve.wait_ge(bd_zero, 1)

            def evacuate(n):
                kind, arg, who = fills[n]
                if who != "D":
                    return
                bank = ps[n % 8]
                dve.wait_ge(filled, n + 1)
                if kind == "ctxT":
                    ins = dve.tensor_copy(ctxT[:, :, :].rearrange("p k m -> p (k m)"), bank[:, 0:DK * B * KEYS])
                elif kind == "k":
                    a0, a1 = arg * PPB, min((arg + 1) * PPB, PAIRS)
                    for j in range(2):
                        rows = slice(j * HD, (j + 1) * HD)
                        ins = dve.tensor_copy(kbd[rows, a0:a1, :, j, :],
                                              bank[rows, 0:(a1 - a0) * B * KEYS].rearrange(
                                                  "p (a b k) -> p a b k", b=B, k=KEYS))
                elif kind == "v":
                    a0, a1 = arg * PPB, min((arg + 1) * PPB, PAIRS)
                    for j in range(2):
                        rows = slice(j * HD, (j + 1) * HD)
                        for b in range(B):
                            ins = dve.tensor_tensor(
                                vb[b][rows, a0:a1, OFF + j * KEYS:OFF + (j + 1) * KEYS],
                                bank[rows, 0:(a1 - a0) * B * KEYS].rearrange(
                                    "p (a b k) -> p a b k", b=B, k=KEYS)[:, :, b, :],
                                vsc[rows, b, :].unsqueeze(1).to_broadcast([HD, a1 - a0, KEYS]), ALU.mult)
                elif kind == "a":
                    b, k, g = arg
                    h0, nh = BANKS[g]
                    cols = slice(h0 * KEYS, (h0 + nh) * KEYS)
                    dve.wait_ge(hi_done, his[n])
                    ins = dve.scalar_tensor_tensor(al[:, b, k, cols], bank[:, 0:nh * KEYS], SC_A / HD ** 0.5,
                                                   ah[:, b, k, cols], ALU.mult, ALU.subtract)
                elif kind == "x":
                    m = slice(2 * arg * P, (2 * arg + 2) * P)
                    dve.wait_ge(hi_done, his[n])
                    ins = dve.tensor_tensor(xtl[:, :, m], bank[:, :].rearrange("p (k m) -> p k m", k=DK),
                                            xth[:, :, m], ALU.subtract)
                elif kind == "vw":
                    b, i = arg
                    dve.wait_ge(hi_done, his[n])
                    ins = dve.tensor_tensor(vwl[:, b, 2 * i:2 * i + 2, :].rearrange("p c d -> p (c d)"), bank[:, :],
                                            vwh[:, b, 2 * i:2 * i + 2, :].rearrange("p c d -> p (c d)"),
                                            ALU.subtract)
                ins.then_inc(dve_out, 1)

            for n in range(of_kind["a"][0]):
                evacuate(n)
            for r in range(2):
                dve.memset(probs[:, r, HK:HKP], 0.0).then_inc(probs_pad, 1)

            def statistics(half):
                h = slice(half * T // 2, (half + 1) * T // 2)
                dve.wait_ge(ld_x[half], 32)
                for t in range(h.start, h.stop):
                    dve.bn_stats(bst1[:, t, :], xall[:, t, :]).then_inc(ln1_st, 1)
                for t in range(h.start, h.stop):
                    dve.wait_ge(ln1_st, t + 1)
                    dve.bn_aggr(mv[:, t, :], bst1[:, t, :]).then_inc(ln1_mv, 1)
                dve.wait_ge(ln1_mv, h.stop)
                dve.tensor_scalar(rstd1[:, h], mv[:, h, 1], EPS, None, ALU.add).then_inc(ln1_ve, 1)

            def shift(half):
                h = slice(half * T // 2, (half + 1) * T // 2)
                dve.wait_ge(ln1_rs, half + 1)
                dve.scalar_tensor_tensor(nmr1[:, h], mv[:, h, 0], -1.0, rstd1[:, h], ALU.mult, ALU.mult)\
                    .then_inc(ln1_nr, 1)
            statistics(0)
            dve.wait_ge(gate_ok, 1)
            dve.tensor_scalar(vsc[:, :, :].rearrange("p b k -> p (b k)"), ind_b[:, :], gates[:, 2:3], SC_VW,
                              ALU.mult, ALU.mult).then_inc(vsc_ok, 1)
            for i, n in enumerate(of_kind["a"]):
                if i == 2:
                    shift(0)
                if i == 5:
                    statistics(1)
                if i == 9:
                    shift(1)
                evacuate(n)
            dve.wait_ge(vsc_ok, 1)
            for n in range(of_kind["v"][0], len(fills)):
                if n == of_kind["v"][0]:
                    dve.wait_ge(vb_zero, 2)
                evacuate(n)

            def body(s, quad):
                par = quad % 2
                t3, t4, other, r3 = s - 3, s - 4, 1 - par, (quad + 1) % ROWS

                def largest(g):
                    h0, nh = BANKS[g]
                    dve.wait_ge(s_sc, NB * s + g + 1)
                    dve.tensor_reduce(mx[:, h0:h0 + nh],
                                      S[g][:, 0:nh * KEYS].rearrange("p (h k) -> p h k", k=KEYS),
                                      X_AXIS, ALU.max).then_inc(s_mx, 1)

                def negated(g):
                    h0, nh = BANKS[g]
                    dve.wait_ge(s_mx, NB * s + g + 1)
                    dve.tensor_scalar(nb[:, h0:h0 + nh], mx[:, h0:h0 + nh], -1.0 / SC_A, None, ALU.mult)\
                        .then_inc(s_nb, 1)
                if has(s, 0):
                    for g in range(NB - 1):
                        largest(g)
                        negated(g)
                if has(s, 3):
                    dve.wait_ge(s_pv, t3 + 1)
                    dve.wait_ge(ld_xr[other], (t3 - other) * 8 + 16)
                    wait(dve, row_free[r3], (t3 - r3) * (16 // ROWS))
                    dve.scalar_tensor_tensor(row[:, r3, 0:D], O[:, 0:D], 1.0 / (SC_P * SC_VW), xr[:, other, :],
                                             ALU.mult, ALU.add).then_inc(s_x2, 1)
                if has(s, 0):
                    largest(NB - 1)
                if has(s, 3):
                    dve.wait_ge(s_x2, t3 + 1)
                    dve.bn_stats(bst[:, :], row[:, r3, 0:D]).then_inc(s_bs, 1)
                    wait_apart(dve, s_bs, t3 + 1)
                    dve.bn_aggr(mv2[:, :], bst[:, :]).then_inc(s_ag, 1)
                    dve.wait_ge(s_ag, t3 + 1)
                    dve.tensor_scalar(ve2[:, :], mv2[:, 1:2], EPS, None, ALU.add).then_inc(s_ve, 1)
                if has(s, 4):
                    dve.wait_ge(s_ro, t4 + 1)
                    dve.tensor_tensor(sc8[:, :], RS, br_b[:, :], ALU.add).then_inc(s_sb, 1)
                if has(s, 0):
                    negated(NB - 1)
                if has(s, 4):
                    wait_apart(dve, s_sb, t4 + 1)
                    dve.max(top8[:, :], sc8[:, :]).then_inc(s_tp, 1)
                    wait_apart(dve, s_tp, t4 + 1)
                    dve.max_index(idx8[:, :], top8[:, :], sc8[:, :]).then_inc(s_ix, 1)
                if has(s, 3):
                    dve.tensor_scalar(row[:, r3, D + 2:D + 3], row[:, r3, D + 2:D + 3], float(ROWS // B * P), None,
                                      ALU.add).then_inc(ids_ok, 1)
                if has(s, 4):
                    dve.wait_ge(s_ix, t4 + 1)
                    dve.tensor_copy(idxf[:, :], idx8[:, 0:1]).then_inc(s_if, 1)
                    dve.wait_ge(s_if, t4 + 1)
                    dve.tensor_scalar(onehot[:, :], iota8[:, :], idxf[:, 0:1], None, ALU.is_equal)\
                        .then_inc(s_oh, 1)
                if has(s, 3):
                    dve.wait_ge(s_rs, t3 + 1)
                    dve.scalar_tensor_tensor(row[:, r3, D + 1:D + 2], mv2[:, 0:1], -1.0, row[:, r3, D:D + 1],
                                             ALU.mult, ALU.mult).then_inc(s_nr, 1)
                    wait(dve, s_t2, t3)
                    dve.wait_ge(s_nr, t3 + 1)
                    dve.tensor_scalar(xn2[:, :], row[:, r3, 0:D], row[:, r3, D:D + 1], row[:, r3, D + 1:D + 2],
                                      ALU.mult, ALU.add).then_inc(s_xn, 1)
                if isinstance(s, int) and s in LOW_AT:
                    low_of_piece(*LOW_AT[s])

                def low_of_vw(parts):
                    for b, i, n, bank in parts:
                        dve.wait_ge(vw_hi, n + 1)
                        hi, lo = vw_at(i, b)
                        dve.tensor_tensor(lo, bank[:, :], hi, ALU.subtract).then_inc(vw_lo, 1)
                low_of_vw(vw_parts(s)[:-1])
                if has(s, 0):
                    dve.wait_ge(s_ex, NB * (s + 1))
                    dve.reciprocal(rz[:, par, :], z[:, par, :]).then_inc(s_rz, 1)
                low_of_vw(vw_parts(s)[-1:])
                if has(s, 4):
                    dve.wait_ge(s_px, t4 + 1)
                    dve.tensor_tensor_reduce(junk8[:, :], onehot[:, :], RP, 1.0, 0.0, ALU.mult, ALU.add,
                                             rank[:, :]).then_inc(s_rk, 1)
                    dve.tensor_tensor(seen[:, :], seen[:, :], onehot[:, :], ALU.add).then_inc(s_ct, 1)
                    dve.wait_ge(s_rk, t4 + 1)
                    dve.scalar_tensor_tensor(pos[:, quad, :], idxf[:, :], float(CAP), rank[:, :],
                                             ALU.mult, ALU.add).then_inc(s_po, 1)
                if has(s, 1):
                    t = s - 1
                    for g, (c0, n) in enumerate(PTB):
                        dve.wait_ge(s_ph, NB * t + g + 1)
                        dve.scalar_tensor_tensor(ptl[:, other, c0:c0 + n, :].rearrange("p c m -> p (c m)"),
                                                 PT[g][:, 0:n * P], SC_P,
                                                 pth[:, other, c0:c0 + n, :].rearrange("p c m -> p (c m)"),
                                                 ALU.mult, ALU.subtract).then_inc(s_pl, 1)
            steps(dve, body)

            tabn = [0]

            def link(ins):
                tabn[0] += 1
                ins.then_inc(tab, 1)
                dve.wait_ge(tab, tabn[0])
            dve.wait_ge(n_ok, 1)
            v = lambda t, a, b: t[:, 0:a * b].rearrange("p (a b) -> p a b", a=a)
            dve.tensor_tensor(ptab[:, :], RP, ecap[:, :], ALU.add).then_inc(pads_ok, 1)
            dve.scalar_tensor_tensor(ppos[:, :], RP, lane[:, 0:1], ecap[:, :], ALU.add, ALU.add)\
                .then_inc(pads_ok, 1)
            link(dve.tensor_tensor(v(tA, NE, T), RP.unsqueeze(2).to_broadcast([P, NE, T]), k128[:, :, :],
                                   ALU.is_gt))
            link(dve.tensor_reduce(nt_e[:, :], v(tA, NE, T), X_AXIS, ALU.add))
            link(dve.tensor_tensor(v(tA, NE, NE), nt_e[:, :].unsqueeze(1).to_broadcast([P, NE, NE]),
                                   incl[:, :, :], ALU.mult))
            link(dve.tensor_reduce(cum_e[:, :], v(tA, NE, NE), X_AXIS, ALU.add))
            link(dve.tensor_tensor(v(tA, NT, NE), cum_e[:, :].unsqueeze(1).to_broadcast([P, NT, NE]),
                                   jrow[:, :, :], ALU.is_le))
            dve.tensor_reduce(ej[:, :], v(tA, NT, NE), X_AXIS, ALU.add)
            link(dve.tensor_tensor(v(tB, NT, NE), v(tA, NT, NE),
                                   nt_e[:, :].unsqueeze(1).to_broadcast([P, NT, NE]), ALU.mult))
            link(dve.tensor_reduce(sj[:, :], v(tB, NT, NE), X_AXIS, ALU.add))
            dve.tensor_scalar(vj[:, :], ej[:, :], float(NE), float(P), ALU.is_lt, ALU.mult)
            dve.tensor_scalar(epad[:, 4:4 + NT], ej[:, :], float(NE - 1), None, ALU.min)
            link(dve.tensor_tensor(kj[:, :], jrow[:, :, 0], sj[:, :], ALU.subtract))
            link(dve.tensor_tensor(kj[:, :], kj[:, :], vj[:, :], ALU.mult))
            dve.tensor_scalar(etab[:, :], ej[:, :], float(NE - 1), None, ALU.min)
            dve.scalar_tensor_tensor(rtab[:, :], ej[:, :], float(CAP), kj[:, :], ALU.mult, ALU.add)\
                .then_inc(rows_ok, 1)
            digit = lambda d: epad[:, d:d + GROUP * QP].rearrange("p (q g) -> p q g", g=GROUP)[:, :, 0]
            acc = digit(DIGITS - 1)
            for d in range(DIGITS - 2, -1, -1):
                to = qacc[:, d % 2, :] if d else qtab[:, :]
                link(dve.scalar_tensor_tensor(to, acc, float(NE), digit(d), ALU.mult, ALU.add))
                acc = to
            dve.memset(junk8[:, 0:1], 0.0).then_inc(tabs_ok, 1)
            for p in range(LOWS, EARLY):
                low_of_piece(p)

            def fbody(s, quad):
                par = quad % 2
                if fhas(s, 0):
                    wait(dve, f_xt, s - 1)
                    dve.wait_ge(ld_ra[par], (s - par) * 8 + 16)
                    dve.tensor_scalar(xnf[:, par, :], ra[:, par, 0:D], ra[:, par, D:D + 1], ra[:, par, D + 1:D + 2],
                                      ALU.mult, ALU.add).then_inc(f_xn, 1)
                if fhas(s, 5):
                    t, other = s - 5, 1 - par
                    e = dve.value_load(etab[0:1, bass.ds(t, 1)], min_val=0, max_val=NE - 1)
                    dve.wait_ge(f_y, t + 1)
                    if isinstance(s, int) and t == 0:
                        dve.wait_ge(ld_b2, 16)
                    wait(dve, f_yo, t)
                    dve.scalar_tensor_tensor(yb[:, :], ps[6 + other][:, D:2 * D], 1.0 / SC_W2,
                                             b2t[:, :, :].rearrange("p e d -> p (e d)")[:, bass.ds(e * D, D)],
                                             ALU.mult, ALU.add).then_inc(f_t1, 1)
                    dve.wait_ge(ld_rb[other], (t - other) * 8 + 16)
                    wait(dve, f_sc[other], (t - other) * 8)
                    dve.tensor_copy(ids[:, other, :], rb[:, other, D + 2:D + 3]).then_inc(f_id, 1)
                    dve.wait_ge(f_t1, t + 1)
                    dve.scalar_tensor_tensor(yt[:, :], ps[6 + other][:, 0:D], 1.0 / SC_W2, yb[:, :],
                                             ALU.mult, ALU.add).then_inc(f_t2, 1)
                    dve.wait_ge(f_t2, t + 1)
                    dve.scalar_tensor_tensor(yo[:, other, :], yt[:, :], gates[:, 3:4], rb[:, other, 0:D],
                                             ALU.mult, ALU.add).then_inc(f_yo, 1)
                if fhas(s, 1):
                    t = s - 1
                    dve.wait_ge(f_xh, t + 1)
                    dve.tensor_tensor(fxl[:, 1 - par, :, :].rearrange("p k m -> p (k m)"), ps[1 - par][:, 0:D],
                                      fxh[:, 1 - par, :, :].rearrange("p k m -> p (k m)"),
                                      ALU.subtract).then_inc(f_xl, 1)
                if isinstance(s, int) and s - 1 in AT_FSTEP:
                    low_of_piece(AT_FSTEP[s - 1])
                if fhas(s, 2):
                    t = s - 2
                    dve.wait_ge(f_ge, 2 * (t + 1))
                    wait(dve, f_y, t - 1)
                    dve.tensor_copy(hh[:, par, :, :], hid[:, par, :, :]).then_inc(f_hh, 1)
            fsteps(dve, fbody)


_INS = ['x', 'ctx_1024', 'fside_BxS2_0', 'g_xattn', 'g_ffn', 'L0_xattn_Wq', 'L0_xattn_Wk', 'L0_xattn_Wv',
        'L0_xattn_Wo', 'L0_ffn_wr', 'L0_ffn_br', 'L0_ffn_w1', 'L0_ffn_b1', 'L0_ffn_w2', 'L0_ffn_b2']
_OUTS = [((2, 1024, 256), 'float32')]


def kernel(**inputs):
    import numpy as _np
    import concourse.bacc as _bacc
    from concourse import mybir as _mybir
    from concourse.bass_utils import run_bass_kernel_spmd as _run

    nc = _bacc.Bacc("TRN2", target_bir_lowering=False, num_devices=1)
    arrays, args = {}, []
    for name in _INS:
        a = _np.ascontiguousarray(inputs[name])
        arrays[f"in_{name}_dram"] = a
        args.append(nc.dram_tensor(f"in_{name}_dram", a.shape, _mybir.dt.from_np(a.dtype), kind="ExternalInput").ap())
    for i, (shape, dtype) in enumerate(_OUTS):
        dt = _mybir.dt.from_np(_np.dtype(dtype))
        args.append(nc.dram_tensor(f"out_{i}_dram", shape, dt, kind="ExternalOutput").ap())
    gated_cross_attention_then_routed_ffn(nc, *args)
    r = _run(nc, [arrays], core_ids=[0])
    got = tuple(r.results[0][f"out_{i}_dram"] for i in range(len(_OUTS)))
    return got[0]
```
